# Optimizing a Trainium2 kernel written in Bass

```python
import numpy as np
import jax
import jax.numpy as jnp

def _softmax(x, axis=-1):
    return jax.nn.softmax(x, axis=axis)

def _gelu(x):
    return jax.nn.gelu(x, approximate=True)

def _silu(x):
    return jax.nn.silu(x)

def _sigmoid(x):
    return jax.nn.sigmoid(x)

def _layernorm(x, axis=-1, eps=1e-05):
    m = jnp.mean(x, axis=axis, keepdims=True)
    v = jnp.var(x, axis=axis, keepdims=True)
    return (x - m) / jnp.sqrt(v + eps)

def _scatter_add(tgt, idx, src, axis=0):
    return tgt.at[idx].add(src)

def _segment_sum(src, seg, n):
    return jax.ops.segment_sum(src, seg, n)
kernel_name = 'mk_seq_postln_d2_jaxref_r8_32e182'

def setup_inputs(seed: int=0):
    np.random.seed(seed)
    _w = jnp.asarray

    def _L0_attn_setup():
        import jax, jax.numpy as jnp
        import numpy as np
        B, S, D, H = (2, 256, 128, 16)
        HD = D // H
        FF = 512
        NUM_ITERS = 8
        DT = 0.1
        LN_EPS = 1e-05

        def _ln(x, g, b):
            m = jnp.mean(x, axis=-1, keepdims=True)
            v = jnp.var(x, axis=-1, keepdims=True)
            return (x - m) * jax.lax.rsqrt(v + LN_EPS) * g + b

        def _forward(x, qkv_w, qkv_b, out_w, out_b, g_attn, b_attn, g1, b1, g2, b2, w_ctx, w_x, b_inl, ff_w1, ff_b1, ff_w2, ff_b2):
            b, s, d = x.shape
            xn = _ln(x, g_attn, b_attn)
            qkv = (xn @ qkv_w + qkv_b).reshape(b, s, 3, H, HD)
            qkv = jnp.transpose(qkv, (2, 0, 3, 1, 4))
            q, k, v = (qkv[0], qkv[1], qkv[2])
            scores = jnp.einsum('bhqd,bhkd->bhqk', q, k) / np.sqrt(HD).astype(np.float32)
            causal = jnp.triu(jnp.ones((s, s), dtype=bool), 1)
            scores = jnp.where(causal[None, None], -jnp.inf, scores)
            attn_w = jax.nn.softmax(scores, axis=-1)
            attn = jnp.einsum('bhqk,bhkd->bhqd', attn_w, v)
            attn = jnp.transpose(attn, (0, 2, 1, 3)).reshape(b, s, d)
            attn = attn @ out_w + out_b
            x = x + attn
            ctx = attn.reshape(b * s, d)
            xs = _ln(x, g1, b1).reshape(b * s, d)
            vs = jnp.zeros_like(xs)

            def step(carry, _):
                xs, vs = carry
                u = jnp.tanh(ctx @ w_ctx + xs @ w_x + b_inl)
                vn = vs + DT * (u - xs - vs)
                xn_ = xs + DT * vn
                return ((xn_, vn), None)
            (xs, vs), _ = jax.lax.scan(step, (xs, vs), None, length=NUM_ITERS)
            x = x + xs.reshape(b, s, d)
            h = _ln(x, g2, b2)
            h = jax.nn.gelu(h @ ff_w1 + ff_b1, approximate=False)
            x = x + (h @ ff_w2 + ff_b2)
            return x
        key = jax.random.key(seed)
        ks = jax.random.split(key, 16)

        def xav(k, shape):
            lim = np.sqrt(6.0 / (shape[0] + shape[1]))
            return jax.random.uniform(k, shape, minval=-lim, maxval=lim, dtype=jnp.float32)
        return {'x': jax.random.normal(ks[0], (B, S, D), dtype=jnp.float32), 'qkv_w': xav(ks[1], (D, 3 * D)), 'qkv_b': jnp.zeros((3 * D,), jnp.float32), 'out_w': xav(ks[2], (D, D)), 'out_b': jnp.zeros((D,), jnp.float32), 'g_attn': jnp.ones((D,), jnp.float32), 'b_attn': jnp.zeros((D,), jnp.float32), 'g1': jnp.ones((D,), jnp.float32), 'b1': jnp.zeros((D,), jnp.float32), 'g2': jnp.ones((D,), jnp.float32), 'b2': jnp.zeros((D,), jnp.float32), 'w_ctx': xav(ks[3], (D, D)), 'w_x': xav(ks[4], (D, D)), 'b_inl': jnp.zeros((D,), jnp.float32), 'ff_w1': xav(ks[5], (D, FF)), 'ff_b1': jnp.zeros((FF,), jnp.float32), 'ff_w2': xav(ks[6], (FF, D)), 'ff_b2': jnp.zeros((D,), jnp.float32)}
    _L0_attn_in = _L0_attn_setup()

    def _L0_ffn_setup():
        import jax, jax.numpy as jnp
        import numpy as np
        R = 64
        key = jax.random.key(seed)
        k1, k2, k3 = jax.random.split(key, 3)
        B, S, D_IN, D_OUT = (8, 512, 128, 128)
        x = jax.random.normal(k1, (B, S, D_IN), dtype=jnp.float32)
        weight = jax.random.normal(k2, (D_OUT, D_IN), dtype=jnp.float32) * (1.0 / np.sqrt(D_IN))
        disha = jax.random.normal(k3, (R, D_OUT), dtype=jnp.float32) * 0.01
        return {'x': x, 'weight': weight, 'disha': disha}
    _L0_ffn_in = _L0_ffn_setup()

    def _L1_attn_setup():
        import jax, jax.numpy as jnp
        import numpy as np
        B, S, E, H = (4, 256, 128, 16)
        HD = E // H
        key = jax.random.key(seed)
        ks = jax.random.split(key, 5)
        scale = 1.0 / np.sqrt(E)
        x = jax.random.normal(ks[0], (B, S, E), dtype=jnp.float32)
        Wqkv = jax.random.uniform(ks[1], (E, 3 * E), dtype=jnp.float32, minval=-scale, maxval=scale)
        bqkv = jax.random.uniform(ks[2], (3 * E,), dtype=jnp.float32, minval=-scale, maxval=scale)
        Wout = jax.random.uniform(ks[3], (E, E), dtype=jnp.float32, minval=-scale, maxval=scale)
        bout = jax.random.uniform(ks[4], (E,), dtype=jnp.float32, minval=-scale, maxval=scale)
        return {'x': x, 'Wqkv': Wqkv, 'bqkv': bqkv, 'Wout': Wout, 'bout': bout}
    _L1_attn_in = _L1_attn_setup()

    def _L1_ffn_setup():
        import jax, jax.numpy as jnp
        import numpy as np
        HIDDEN = 128
        INTER = 512
        key = jax.random.key(seed)
        k1, k2, k3, k4, k5 = jax.random.split(key, 5)
        hidden_states = jax.random.normal(k1, (4, 256, HIDDEN), dtype=jnp.float32)
        W1 = jax.random.normal(k2, (HIDDEN, INTER), dtype=jnp.float32) * (1.0 / np.sqrt(HIDDEN))
        b1 = jax.random.normal(k3, (INTER,), dtype=jnp.float32) * 0.02
        W2 = jax.random.normal(k4, (INTER, HIDDEN), dtype=jnp.float32) * (1.0 / np.sqrt(INTER))
        b2 = jax.random.normal(k5, (HIDDEN,), dtype=jnp.float32) * 0.02
        return {'hidden_states': hidden_states, 'W1': W1, 'b1': b1, 'W2': W2, 'b2': b2}
    _L1_ffn_in = _L1_ffn_setup()
    _d = {'L0_attn_x': _L0_attn_in['x'], 'L0_attn_qkv_w': _L0_attn_in['qkv_w'], 'L0_attn_qkv_b': _L0_attn_in['qkv_b'], 'L0_attn_out_w': _L0_attn_in['out_w'], 'L0_attn_out_b': _L0_attn_in['out_b'], 'L0_attn_g_attn': _L0_attn_in['g_attn'], 'L0_attn_b_attn': _L0_attn_in['b_attn'], 'L0_attn_g1': _L0_attn_in['g1'], 'L0_attn_b1': _L0_attn_in['b1'], 'L0_attn_g2': _L0_attn_in['g2'], 'L0_attn_b2': _L0_attn_in['b2'], 'L0_attn_w_ctx': _L0_attn_in['w_ctx'], 'L0_attn_w_x': _L0_attn_in['w_x'], 'L0_attn_b_inl': _L0_attn_in['b_inl'], 'L0_attn_ff_w1': _L0_attn_in['ff_w1'], 'L0_attn_ff_b1': _L0_attn_in['ff_b1'], 'L0_attn_ff_w2': _L0_attn_in['ff_w2'], 'L0_attn_ff_b2': _L0_attn_in['ff_b2'], 'L0_ffn_weight': _L0_ffn_in['weight'], 'L0_ffn_disha': _L0_ffn_in['disha'], 'L1_attn_Wqkv': _L1_attn_in['Wqkv'], 'L1_attn_bqkv': _L1_attn_in['bqkv'], 'L1_attn_Wout': _L1_attn_in['Wout'], 'L1_attn_bout': _L1_attn_in['bout'], 'L1_ffn_W1': _L1_ffn_in['W1'], 'L1_ffn_b1': _L1_ffn_in['b1'], 'L1_ffn_W2': _L1_ffn_in['W2'], 'L1_ffn_b2': _L1_ffn_in['b2']}
    _x0 = _d['L0_attn_x']
    _d['L0_attn_x'] = jax.random.normal(jax.random.fold_in(jax.random.key(seed), 1), (4, 1024, 128), dtype=_x0.dtype)
    del _x0
    return _d

def reference(L0_attn_x, L0_attn_qkv_w, L0_attn_qkv_b, L0_attn_out_w, L0_attn_out_b, L0_attn_g_attn, L0_attn_b_attn, L0_attn_g1, L0_attn_b1, L0_attn_g2, L0_attn_b2, L0_attn_w_ctx, L0_attn_w_x, L0_attn_b_inl, L0_attn_ff_w1, L0_attn_ff_b1, L0_attn_ff_w2, L0_attn_ff_b2, L0_ffn_weight, L0_ffn_disha, L1_attn_Wqkv, L1_attn_bqkv, L1_attn_Wout, L1_attn_bout, L1_ffn_W1, L1_ffn_b1, L1_ffn_W2, L1_ffn_b2):

    def _L0_attn_ref(x, qkv_w, qkv_b, out_w, out_b, g_attn, b_attn, g1, b1, g2, b2, w_ctx, w_x, b_inl, ff_w1, ff_b1, ff_w2, ff_b2):
        import jax, jax.numpy as jnp
        import numpy as np
        B, S, D, H = (2, 256, 128, 16)
        HD = D // H
        FF = 512
        NUM_ITERS = 8
        DT = 0.1
        LN_EPS = 1e-05

        def _ln(x, g, b):
            m = jnp.mean(x, axis=-1, keepdims=True)
            v = jnp.var(x, axis=-1, keepdims=True)
            return (x - m) * jax.lax.rsqrt(v + LN_EPS) * g + b

        def _forward(x, qkv_w, qkv_b, out_w, out_b, g_attn, b_attn, g1, b1, g2, b2, w_ctx, w_x, b_inl, ff_w1, ff_b1, ff_w2, ff_b2):
            b, s, d = x.shape
            xn = _ln(x, g_attn, b_attn)
            qkv = (xn @ qkv_w + qkv_b).reshape(b, s, 3, H, HD)
            qkv = jnp.transpose(qkv, (2, 0, 3, 1, 4))
            q, k, v = (qkv[0], qkv[1], qkv[2])
            scores = jnp.einsum('bhqd,bhkd->bhqk', q, k) / np.sqrt(HD).astype(np.float32)
            causal = jnp.triu(jnp.ones((s, s), dtype=bool), 1)
            scores = jnp.where(causal[None, None], -jnp.inf, scores)
            attn_w = jax.nn.softmax(scores, axis=-1)
            attn = jnp.einsum('bhqk,bhkd->bhqd', attn_w, v)
            attn = jnp.transpose(attn, (0, 2, 1, 3)).reshape(b, s, d)
            attn = attn @ out_w + out_b
            x = x + attn
            ctx = attn.reshape(b * s, d)
            xs = _ln(x, g1, b1).reshape(b * s, d)
            vs = jnp.zeros_like(xs)

            def step(carry, _):
                xs, vs = carry
                u = jnp.tanh(ctx @ w_ctx + xs @ w_x + b_inl)
                vn = vs + DT * (u - xs - vs)
                xn_ = xs + DT * vn
                return ((xn_, vn), None)
            (xs, vs), _ = jax.lax.scan(step, (xs, vs), None, length=NUM_ITERS)
            x = x + xs.reshape(b, s, d)
            h = _ln(x, g2, b2)
            h = jax.nn.gelu(h @ ff_w1 + ff_b1, approximate=False)
            x = x + (h @ ff_w2 + ff_b2)
            return x
        return _forward(x, qkv_w, qkv_b, out_w, out_b, g_attn, b_attn, g1, b1, g2, b2, w_ctx, w_x, b_inl, ff_w1, ff_b1, ff_w2, ff_b2)

    def _L0_ffn_ref(x, weight, disha):
        import jax, jax.numpy as jnp
        import numpy as np
        R = 64
        result = jnp.einsum('bsd,od->bso', x, weight)
        r = disha.shape[0]
        pooled = x.reshape(*x.shape[:-1], x.shape[-1] // r, r).sum(axis=-2)
        return result + pooled @ disha

    def _L1_attn_ref(x, Wqkv, bqkv, Wout, bout):
        import jax, jax.numpy as jnp
        import numpy as np
        B, S, E, H = (4, 256, 128, 16)
        HD = E // H
        b, s, e = x.shape
        qkv = x @ Wqkv + bqkv
        qkv = qkv.reshape(b, s, H, 3 * HD)
        q, k, v = (qkv[..., :HD], qkv[..., HD:2 * HD], qkv[..., 2 * HD:])
        scores = jnp.einsum('bqhd,bkhd->bhqk', q, k) / jnp.sqrt(jnp.float32(HD))
        attn = jax.nn.softmax(scores, axis=-1)
        out = jnp.einsum('bhqk,bkhd->bqhd', attn, v).reshape(b, s, e)
        return out @ Wout + bout

    def _L1_ffn_ref(hidden_states, W1, b1, W2, b2):
        import jax, jax.numpy as jnp
        import numpy as np
        HIDDEN = 128
        INTER = 512
        h = jax.nn.relu(jnp.einsum('bsh,hi->bsi', hidden_states, W1) + b1)
        return jnp.einsum('bsi,ih->bsh', h, W2) + b2
    x = L0_attn_x
    x = _layernorm(x + _L0_attn_ref(x, L0_attn_qkv_w, L0_attn_qkv_b, L0_attn_out_w, L0_attn_out_b, L0_attn_g_attn, L0_attn_b_attn, L0_attn_g1, L0_attn_b1, L0_attn_g2, L0_attn_b2, L0_attn_w_ctx, L0_attn_w_x, L0_attn_b_inl, L0_attn_ff_w1, L0_attn_ff_b1, L0_attn_ff_w2, L0_attn_ff_b2), axis=-1)
    x = _layernorm(x + _L0_ffn_ref(x, L0_ffn_weight, L0_ffn_disha), axis=-1)
    x = _layernorm(x + _L1_attn_ref(x, L1_attn_Wqkv, L1_attn_bqkv, L1_attn_Wout, L1_attn_bout), axis=-1)
    x = _layernorm(x + _L1_ffn_ref(x, L1_ffn_W1, L1_ffn_b1, L1_ffn_W2, L1_ffn_b2), axis=-1)
    return x

_drawn_inputs = setup_inputs


def setup_inputs(seed=0):
    import zlib

    import numpy as np

    out = dict(_drawn_inputs(seed))
    spreads = {'L0_attn_qkv_b': (0.0, 0.1),
     'L0_attn_out_b': (0.0, 0.1),
     'L0_attn_g_attn': (1.0, 0.6),
     'L0_attn_b_attn': (0.0, 0.1),
     'L0_attn_g1': (1.0, 0.2),
     'L0_attn_b1': (0.0, 0.271),
     'L0_attn_g2': (1.0, 0.2),
     'L0_attn_b2': (0.0, 0.416),
     'L0_attn_b_inl': (0.0, 0.8),
     'L0_attn_ff_b1': (0.0, 0.296),
     'L0_attn_ff_b2': (0.0, 0.268)}
    factors = {'L0_attn_w_ctx': 4.26, 'L1_ffn_b1': 4.999, 'L1_ffn_b2': 3.447}
    for name, (base, spread) in spreads.items():
        noise = np.random.default_rng([zlib.crc32(name.encode()), seed]).standard_normal(out[name].shape)
        drawn = base * np.exp(spread * noise) if base else spread * noise
        out[name] = jnp.asarray(drawn.astype(out[name].dtype))
    for name, factor in factors.items():
        out[name] = (out[name] * factor).astype(out[name].dtype)
    return out
```

```python
import concourse.bass as bass
from concourse import mybir
from contextlib import ExitStack

F32 = mybir.dt.float32
BF16 = mybir.dt.bfloat16
ALU = mybir.AluOpType
ACT = mybir.ActivationFunctionType
AX_X = mybir.AxisListType.X

P = 128
B, SEQ, D = 4, 1024, 128
H, HD = 16, 8
FF = 512
ITERS = 8
DT = 0.1
EPS = 1e-5
TOK = B * SEQ
TILES = TOK // P
BANK = 512
CH = 512
CT = CH // P
NCH = 4
NLOOP = TOK // (CH * NCH)

QPART = (0, 0, 0, 1, 1, 2)
KPART = (0, 1, 2, 0, 1, 0)
NPROD = len(QPART)
ROWS = NPROD * HD
MROW = 96
GH = 4
NG = H // GH
QT = SEQ // P
QH = SEQ // CH
SCALE = 1.0 / float(HD) ** 0.5

W_AT = {}
_at = 0
for _n, _w in (("q0", D), ("k0", D), ("v0", D), ("o0", D), ("ctx", D), ("x", D), ("f1", FF), ("f2", FF),
               ("lin", D), ("dis", D), ("q1", D), ("k1", D), ("v1", D), ("o1", D), ("g1", FF), ("g2", FF)):
    W_AT[_n] = (_at, _w)
    _at += _w
W_COLS = _at
C_AT = {n: i for i, n in enumerate(
    ("bq0", "bk0", "bo0", "g_attn", "b_attn", "g1", "b1", "g2", "b2", "b_inl", "f0", "f1", "f2", "f3",
     "bq1", "bk1", "h0", "h1", "h2", "h3"))}
R_AT = {n: i for i, n in enumerate(("bv0", "fb2", "bv1", "bo1", "hb2"))}


def chunk_tiles(it, c):
    return bass.ds((it * NCH + c) * CT, CT)


def attention_steps(causal):
    return [(qh, kt, max(0, kt * P - qh * CH) if causal else 0) for qh in range(QH) for kt in range(QT)
            if not causal or kt * P < (qh + 1) * CH]


def score_units(causal):
    out = []
    for h in range(GH):
        for qt in range(QT):
            keys = (qt + 1) * P if causal else SEQ
            out += [(h, qt, n, at, min(BANK, keys - at)) for n, at in enumerate(range(0, keys, BANK))]
    return out



def stage_semaphores(nc, ctx, prefix, taken):
    def sem(n):
        taken.append(ctx.enter_context(nc.semaphore(f"{prefix}_{n}")))
        return taken[-1]
    return sem


def retire(nc, taken):
    with nc.Block() as block:
        @block.sync
        def _(sp):
            for s in taken:
                sp.sem_clear(s)


def attention(nc, taken, name, causal, scr_q, scr_k, scr_m, v_tm, attn_tm, ident, mask_neg, ident_bf):
    steps = attention_steps(causal)
    units = score_units(causal)
    NS, NU = len(steps), len(units)
    first_of = [min(n for n, s in enumerate(steps) if s[0] == qh) for qh in range(QH)]
    last_of = [max(n for n, s in enumerate(steps) if s[0] == qh) for qh in range(QH)]
    heads_of = [((0, 1, 2, 3),) if CH - lo <= BANK // 2 else ((0, 1), (2, 3)) for _, _, lo in steps]
    exp_before = [sum(len(x) for x in heads_of[:n]) for n in range(NS + 1)]
    NE = exp_before[NS]
    diagonal = [causal and kt * P >= qh * CH for qh, kt, _ in steps]
    ND = sum(diagonal)
    PRING = 4
    assert NE % 2 == 0 and NU % 2 == 0 and NS % PRING == 0
    TAIL = 4
    cut = [(NU - TAIL) * n // NS for n in range(NS + 1)]
    LOADS = 2 * 16

    with ExitStack() as ctx:
        def sb(n, shape, dt):
            return ctx.enter_context(nc.sbuf_tensor(f"{name}_{n}", shape, dt))

        sem = stage_semaphores(nc, ctx, name, taken)
        Qs = [sb(f"Qs{i}", [P, GH, SEQ], BF16) for i in range(NG)]
        Ks = [sb(f"Ks{i}", [P, GH, SEQ], BF16) for i in range(NG)]
        pT = [sb(f"pT{i}", [P, GH, CH], F32) for i in range(PRING)]
        vs = [sb(f"vs{i}", [P, QT, GH, 32], F32) for i in range(2)]
        negp = [sb(f"negp{i}", [P, GH * QT, 2], F32) for i in range(2)]
        negm = sb("negm", [P, GH * QT], F32)
        msp = sb("msp", [GH * QT, 3, P], BF16)
        mres = sb("mres", [GH * QT, 2, P], F32)
        outT = sb("outT", [P, CH], F32)
        rc = sb("rc", [P, CT, GH], F32)
        held = sb("held", [P, 2], F32)
        ps = ctx.enter_context(nc.psum_tensor(f"{name}_ps", [P, 8 * BANK], F32))
        s_ps = [ps[:, n * BANK:(n + 1) * BANK] for n in range(2)]
        st_ps = [ps[:, (2 + 2 * n) * BANK:(4 + 2 * n) * BANK] for n in range(2)]
        pv_ps = ps[:, 6 * BANK:7 * BANK]
        t_ps = ps[:, 7 * BANK:8 * BANK]

        cleared = sem("cleared")
        ones_set = sem("ones_set")
        negp_set = sem("negp_set")
        loaded = [sem(f"loaded{i}") for i in range(NG)]
        max_rows = [sem(f"max_rows{i}") for i in range(NG)]
        scored = sem("scored")
        reduced = sem("reduced")
        keyed = sem("keyed")
        exped = sem("exped")
        masked = sem("masked")
        weighed = sem("weighed")
        evacuated = sem("evacuated")
        turned = sem("turned")
        recips = sem("recips")
        normed = sem("normed")
        max_joined = sem("max_joined")
        max_turned = sem("max_turned")
        max_part = sem("max_part")
        max_split = sem("max_split")
        max_stored = sem("max_stored")
        v_clear = sem("v_clear")
        v_ready = sem("v_ready")
        block = ctx.enter_context(nc.Block())

        @block.sync
        def _(sp):
            def load(b, u):
                for scr, slot in ((scr_q, Qs[u]), (scr_k, Ks[u])):
                    sp.dma_start(slot[0:ROWS, :, :],
                                 scr[:, u * GH:(u + 1) * GH, bass.ds(b * SEQ, SEQ)]).then_inc(loaded[u], 16)

            def put_max(g, u):
                sp.wait_ge(max_split, g + 1)
                mine = scr_m[:, bass.ds(g * GH * QT, GH * QT), :]
                sp.dma_start(mine.rearrange("s r c -> r s c"), msp[:, :, :]).then_inc(max_stored, 16)
                sp.wait_ge(max_stored, 16 * (g + 1))
                sp.dma_start(Qs[u][MROW:MROW + 3, :, :].rearrange("p h (t c) -> p (h t) c", c=P), mine)\
                    .then_inc(max_rows[u], 16)

            def body(b, u, ahead):
                g = NG * b + u
                if ahead >= 3:
                    sp.wait_ge(keyed, NE * g)
                    load(b + (u + 3) // NG, (u + 3) % NG)
                if ahead >= 1:
                    put_max(g + 1, (u + 1) % NG)

            sp.wait_ge(cleared, 2 * NG)
            for u in range(3):
                load(0, u)
            sp.wait_ge(ones_set, 2 * NG)
            put_max(0, 0)
            with sp.Fori(0, B - 1) as b:
                for u in range(NG):
                    body(b, u, NG)
            for u in range(NG):
                body(B - 1, u, NG - 1 - u)

        @block.gpsimd
        def _(pool):
            def values(b, u):
                pool.tensor_copy(vs[u % 2][:, :, :, 0:HD],
                                 v_tm[:, bass.ds(b * QT, QT), u * GH * HD:(u + 1) * GH * HD]
                                 .rearrange("p t (h d) -> p t h d", d=HD)).then_inc(v_ready, 1)

            def body(b, u, more):
                g = NG * b + u
                if more:
                    pool.wait_ge(weighed, NS * g)
                    values(b + (u + 1) // NG, (u + 1) % NG)
                for n, (qh, kt, lo) in enumerate(steps):
                    if diagonal[n]:
                        pool.wait_ge(masked, ND * g + sum(diagonal[:n]))
                        pool.wait_ge(exped, NE * g + exp_before[n + 1])
                        pool.tensor_tensor(held[:, 0:1], held[:, 1:2], held[:, 1:2], ALU.mult)
                        blk = pT[n % PRING][:, :, lo:lo + P]
                        pool.affine_select(out=blk, in_=blk, compare_op=ALU.is_ge, fill=0.0, base=0,
                                           pattern=[[0, GH], [1, P]], channel_multiplier=-1)\
                            .then_inc(masked, 1)

            pool.memset(held[:, :], 0.0)
            for i in range(2):
                pool.memset(vs[i][:, :, :, :], 0.0).then_inc(v_clear, 1)
            pool.wait_ge(v_clear, 2)
            for i in range(2):
                pool.memset(vs[i][:, :, :, HD:HD + 1], 1.0).then_inc(v_clear, 1)
            pool.wait_ge(v_clear, 4)
            values(0, 0)
            with pool.Fori(0, B - 1) as b:
                for u in range(NG):
                    body(b, u, True)
            for u in range(NG):
                body(B - 1, u, u < NG - 1)

        @block.scalar
        def _(act):
            def evacuate(g, qh):
                act.wait_ge(weighed, NS * g + last_of[qh] + 1)
                act.wait_ge(turned, QH * g + qh)
                act.activation(outT[:, :], pv_ps, ACT.Copy).then_inc(evacuated, 1)

            def body(b, u):
                g = NG * b + u
                for n, (qh, kt, lo) in enumerate(steps):
                    act.wait_ge(weighed, NS * g + (n - PRING + 1 if u else max(n - PRING + 1, 0)))
                    for e, hs in enumerate(heads_of[n]):
                        k = exp_before[n] + e
                        act.wait_ge(keyed, NE * g + k + 1)
                        src = st_ps[k % 2].rearrange("p (h c) -> p h c", h=len(hs))[:, :, 0:CH - lo]
                        act.activation(pT[n % PRING][:, hs[0]:hs[-1] + 1, lo:CH], src, ACT.Exp, scale=SCALE)\
                            .then_inc(exped, 1)
                    if n == first_of[1]:
                        evacuate(g, 0)
                evacuate(g, 1)

            with act.Fori(0, B) as b:
                for u in range(NG):
                    body(b, u)

        @block.vector
        def _(dve):
            def reduce(g, par, k):
                h, qt, part, at, w = units[k]
                dve.wait_ge(scored, NU * g + k + 1)
                dve.tensor_reduce(negp[par][:, h * QT + qt, part:part + 1], s_ps[k % 2][:, 0:w],
                                  AX_X, ALU.max, negate=True).then_inc(reduced, 1)

            def join(g, par):
                dve.wait_ge(reduced, NU * (g + 1))
                dve.wait_ge(max_turned, g)
                dve.tensor_tensor(negm[:, :], negp[par][:, :, 0], negp[par][:, :, 1], ALU.min)\
                    .then_inc(max_joined, 1)

            def split(g):
                src = t_ps[0:GH * QT, 0:P]
                dve.wait_ge(max_turned, g + 1)
                dve.wait_ge(max_stored, 16 * g)
                dve.tensor_copy(msp[:, 0, :], src).then_inc(max_part, 1)
                dve.wait_ge(max_part, 4 * g + 1)
                dve.tensor_tensor(mres[:, 0, :], src, msp[:, 0, :], ALU.subtract).then_inc(max_part, 1)
                dve.wait_ge(max_part, 4 * g + 2)
                dve.tensor_copy(msp[:, 1, :], mres[:, 0, :]).then_inc(max_part, 1)
                dve.wait_ge(max_part, 4 * g + 3)
                dve.tensor_tensor(mres[:, 1, :], mres[:, 0, :], msp[:, 1, :], ALU.subtract).then_inc(max_part, 1)
                dve.wait_ge(max_part, 4 * g + 4)
                dve.tensor_copy(msp[:, 2, :], mres[:, 1, :]).then_inc(max_split, 1)

            def norm(b, u, g, qh):
                src = t_ps.rearrange("p (t h c) -> p t h c", t=CT, h=GH)
                dve.wait_ge(turned, QH * g + qh + 1)
                dve.reciprocal(rc[:, :, :], src[:, :, :, HD]).then_inc(recips, 1)
                dve.wait_ge(recips, QH * g + qh + 1)
                dst = attn_tm[:, bass.ds(b * QT + qh * CT, CT), u * GH * HD:(u + 1) * GH * HD]
                dve.tensor_tensor(dst.rearrange("p t (h d) -> p t h d", d=HD), src[:, :, :, 0:HD],
                                  rc[:, :, :].unsqueeze(3).to_broadcast([P, CT, GH, HD]), ALU.mult)\
                    .then_inc(normed, 1)

            def body(b, u, ahead):
                g = NG * b + u
                if ahead >= 1:
                    join(g + 1, (u + 1) % 2)
                for n in range(NS):
                    if n == 2 and ahead >= 1:
                        split(g + 1)
                    if n == first_of[1] + 2:
                        norm(b, u, g, 0)
                    if ahead >= 2:
                        for k in range(cut[n], cut[n + 1]):
                            reduce(g + 2, u % 2, k)
                if ahead >= 2:
                    for k in range(cut[NS], NU):
                        reduce(g + 2, u % 2, k)
                norm(b, u, g, 1)

            for u in range(NG):
                dve.memzero(Qs[u][:, :, :]).then_inc(cleared, 1)
                dve.memzero(Ks[u][:, :, :]).then_inc(cleared, 1)
            for i in range(2):
                dve.memset(negp[i][:, :, 1], 3.0e38).then_inc(negp_set, 1)
            dve.wait_ge(cleared, 2 * NG)
            for u in range(NG):
                dve.memset(Ks[u][MROW:MROW + 3, :, :], 1.0).then_inc(ones_set, 2)
            dve.wait_ge(negp_set, 2)
            for g in range(2):
                for k in range(NU):
                    reduce(g, g, k)
                if g == 0:
                    join(0, 0)
                    split(0)
            with dve.Fori(0, B - 1) as b:
                for u in range(NG):
                    body(b, u, NG)
            for u in range(NG):
                body(B - 1, u, NG - 1 - u)

        @block.tensor
        def _(pe):
            def score(g, s, k):
                h, qt, part, at, w = units[k]
                n = NU * g + k - 1
                if not isinstance(n, int) or n > 0:
                    pe.wait_ge(reduced, n)
                out = s_ps[k % 2][:, 0:w]
                diag = causal and at + w == (qt + 1) * P
                last = pe.matmul(out, Qs[s][0:MROW, h, qt * P:(qt + 1) * P], Ks[s][0:MROW, h, at:at + w],
                                 start=True, stop=True)
                if diag:
                    last = pe.matmul(out[:, w - P:w], ident_bf, mask_neg, start=False, stop=True,
                                     skip_group_check=True)
                last.then_inc(scored, 1)

            def key_scores(g, u, n):
                qh, kt, lo = steps[n]
                w = CH - lo
                for e, hs in enumerate(heads_of[n]):
                    k = exp_before[n] + e
                    if u or k >= 1:
                        pe.wait_ge(exped, NE * g + k - 1)
                    elif not isinstance(g, int):
                        pe.wait_ge(exped, NE * g)
                    out = st_ps[k % 2].rearrange("p (h c) -> p h c", h=len(hs))
                    for i, h in enumerate(hs):
                        last = pe.matmul(out[:, i, 0:w], Ks[u][:, h, kt * P:(kt + 1) * P],
                                         Qs[u][:, h, qh * CH + lo:(qh + 1) * CH], start=True, stop=True)
                    last.then_inc(keyed, 1)

            def weigh(g, u, n):
                qh, kt, lo = steps[n]
                pe.wait_ge(exped, NE * g + exp_before[n + 1])
                if diagonal[n]:
                    pe.wait_ge(masked, ND * g + sum(diagonal[:n + 1]))
                if n == first_of[qh]:
                    pe.wait_ge(evacuated, QH * g + qh)
                for h in range(GH):
                    last = pe.matmul(pv_ps[32 * h:32 * h + 32, lo:CH], vs[u % 2][:, kt, h, :],
                                     pT[n % PRING][:, h, lo:CH], start=n == first_of[qh], stop=True,
                                     skip_group_check=True)
                last.then_inc(weighed, 1)

            def turn_max(g):
                pe.wait_ge(max_joined, g + 1)
                pe.wait_ge(normed, QH * (g - 1) if not isinstance(g, int) or g else 0)
                pe.transpose(t_ps[0:GH * QT, 0:P], negm[:, :], ident).then_inc(max_turned, 1)

            def turn_out(g, qh, splits):
                pe.wait_ge(evacuated, QH * g + qh + 1)
                pe.wait_ge(max_split, splits)
                pe.wait_ge(normed, QH * g + qh)
                for t in range(CT):
                    last = pe.transpose(t_ps[:, t * P:(t + 1) * P], outT[:, t * P:(t + 1) * P], ident)
                last.then_inc(turned, 1)

            def body(b, u, ahead):
                g = NG * b + u
                splits = g + 2 if ahead >= 1 else g + 1
                pe.wait_ge(max_rows[u], 16 * (b + 1))
                pe.wait_ge(v_ready, g + 1)
                s = (u + 2) % NG
                if ahead >= 2:
                    pe.wait_ge(loaded[s], LOADS * (b + (u + 2) // NG + 1))
                for n in range(NS):
                    key_scores(g, u, n)
                    if ahead >= 2:
                        for k in range(cut[n], cut[n + 1]):
                            score(g + 2, s, k)
                    if n == 1 and ahead >= 1:
                        turn_max(g + 1)
                    if n:
                        weigh(g, u, n - 1)
                    if n == first_of[1] + 1:
                        turn_out(g, 0, splits)
                if ahead >= 2:
                    for k in range(cut[NS], NU):
                        score(g + 2, s, k)
                weigh(g, u, NS - 1)
                turn_out(g, 1, splits)

            pe.wait_ge(ones_set, 2 * NG)
            for g in range(2):
                pe.wait_ge(loaded[g], LOADS)
                for k in range(NU):
                    score(g, g, k)
                if g == 0:
                    turn_max(0)
            with pe.Fori(0, B - 1) as b:
                for u in range(NG):
                    body(b, u, NG)
            for u in range(NG):
                body(B - 1, u, NG - 1 - u)


class Norm:

    def __init__(self, ctx, nc, taken, name, roots):
        def sb(n, shape):
            return ctx.enter_context(nc.sbuf_tensor(f"{name}_{n}", shape, F32))

        sem = stage_semaphores(nc, ctx, name, taken)

        self.eps, self.neg_half = roots
        self.bst, self.mv = sb("bst", [P, NCH, CT, 6]), sb("mv", [P, NCH, CT, 2])
        self.ve, self.rs = sb("ve", [P, NCH, CT]), sb("rs", [P, NCH, CT])
        self.stats_in, self.mean_var, self.eps_added, self.rooted, self.done = (
            sem(n) for n in ("stats_in", "mean_var", "eps_added", "rooted", "done"))

    def on_vector(self, dve, n0, before, src, dst):
        def stats(c):
            for t in range(CT):
                last = dve.bn_stats(self.bst[:, c, t, :], src(c)[:, t, :])
            last.then_inc(self.stats_in, 1)

        def mean(c):
            for t in range(CT):
                last = dve.bn_aggr(self.mv[:, c, t, :], self.bst[:, c, t, :])
            last.then_inc(self.mean_var, 1)

        def scale(c):
            dve.wait_ge(self.rooted, n0 + c + 1)
            for t in range(CT):
                last = dve.tensor_scalar(dst(c)[:, t, :], src(c)[:, t, :], self.mv[:, c, t, 0:1],
                                         self.rs[:, c, t:t + 1], ALU.subtract, ALU.mult)
            last.then_inc(self.done, 1)

        for c in range(NCH):
            if c >= 2:
                dve.wait_ge(self.stats_in, n0 + c - 1)
            before(c)
            stats(c)
            if c >= 2:
                mean(c - 2)
        for c in range(NCH):
            if c < 2:
                dve.wait_ge(self.stats_in, n0 + NCH - 1 + c)
            scale(c)
            if c < 2:
                mean(NCH - 2 + c)

    def root(self, pool, n, c):
        pool.wait_ge(self.mean_var, n + 1)
        pool.tensor_tensor(self.ve[:, c, :], self.mv[:, c, :, 1], self.eps[:, 0:CT], ALU.add)\
            .then_inc(self.eps_added, 1)
        pool.wait_ge(self.eps_added, n + 1)
        pool.tensor_tensor(self.rs[:, c, :], self.ve[:, c, :], self.neg_half[:, 0:CT], ALU.pow)\
            .then_inc(self.rooted, 1)


def turn(pe, bank, src, ident):
    for t in range(CT):
        last = pe.transpose(bank[:, t * P:(t + 1) * P], src[:, t * P:(t + 1) * P], ident)
    return last


def tokens_out(pe, bank, src, weight):
    for t in range(CT):
        last = pe.matmul(bank[:, t * P:(t + 1) * P], src[:, t * P:(t + 1) * P], weight, start=True, stop=True)
    return last


class Qkv:

    def __init__(self, ctx, nc, taken, name, wq, wk, wv, bq, bk, bv, scr_q, scr_k, v_tm, x32):
        def sb(n, shape, dt):
            return ctx.enter_context(nc.sbuf_tensor(f"{name}_{n}", shape, dt))

        sem = stage_semaphores(nc, ctx, name, taken)

        self.w, self.wv = (wq, wk), wv
        self.b, self.bv, self.scr, self.v_tm, self.x32 = (bq, bk), bv, (scr_q, scr_k), v_tm, x32
        self.part = [sb(f"part{i}", [P, NCH, 3, CH], BF16) for i in range(2)]
        self.mm = [sem("q_mm"), sem("k_mm")]
        self.ev = [sem("q_ev"), sem("k_ev")]
        self.first = [sem("q_first"), sem("k_first")]
        self.rest1 = [sem("q_rest1"), sem("k_rest1")]
        self.second = [sem("q_second"), sem("k_second")]
        self.parted = [sem("q_parted"), sem("k_parted")]
        self.v_mm, self.v_ev = sem("v_mm"), sem("v_ev")
        self.written = [sem(f"written{c}") for c in range(NCH)]

    def pe(self, pe, it, ready, src, bank):
        for s in range(2):
            for c in range(NCH):
                n = NCH * it + c
                if s == 0:
                    pe.wait_ge(ready, n + 1)
                if s == 0:
                    pe.wait_ge(self.v_ev, NCH * it)
                pe.matmul(bank[4 + c if s == 0 else c], self.w[s], src[:, c, :], start=True, stop=True)\
                    .then_inc(self.mm[s], 1)
        for c in range(NCH):
            pe.wait_ge(self.ev[0], NCH * it + c + 1)
            tokens_out(pe, bank[4 + c], src[:, c, :], self.wv).then_inc(self.v_mm, 1)

    def act(self, act, it, bank):
        for s in range(2):
            for c in range(NCH):
                n = NCH * it + c
                act.wait_ge(self.mm[s], n + 1)
                act.wait_ge(self.parted[s], NCH * it)
                act.activation(self.x32[s][:, c, :], bank[4 + c if s == 0 else c], ACT.Identity, bias=self.b[s])\
                    .then_inc(self.ev[s], 1)
        for s in range(2):
            for c in range(NCH):
                act.wait_ge(self.ev[s], NCH * it + c + 1)
                act.wait_ge(self.written[c], 2 * NPROD * 16 * it)
                act.activation(self.part[s][:, c, 0, :], self.x32[s][:, c, :], ACT.Copy)\
                    .then_inc(self.first[s], 1)
        for s in range(2):
            for c in range(NCH):
                act.wait_ge(self.rest1[s], NCH * it + c + 1)
                act.activation(self.part[s][:, c, 1, :], self.x32[s][:, c, :], ACT.Copy)\
                    .then_inc(self.second[s], 1)

    def rest(self, eng, s, it):
        for c in range(NCH):
            eng.wait_ge(self.first[s], NCH * it + c + 1)
            eng.tensor_tensor(self.x32[s][:, c, :], self.x32[s][:, c, :], self.part[s][:, c, 0, :], ALU.subtract)\
                .then_inc(self.rest1[s], 1)
        for c in range(NCH):
            eng.wait_ge(self.second[s], NCH * it + c + 1)
            eng.tensor_tensor(self.part[s][:, c, 2, :], self.x32[s][:, c, :], self.part[s][:, c, 1, :],
                              ALU.subtract).then_inc(self.parted[s], 1)

    def values(self, dve, it, bank):
        for c in range(NCH):
            dve.wait_ge(self.v_mm, NCH * it + c + 1)
            dve.tensor_tensor(self.v_tm[:, chunk_tiles(it, c), :], bank[4 + c].rearrange("p (t f) -> p t f", f=P),
                              self.bv.unsqueeze(1).to_broadcast([P, CT, P]), ALU.add).then_inc(self.v_ev, 1)

    def write(self, sp, it):
        for c in range(NCH):
            for s, order in enumerate((QPART, KPART)):
                sp.wait_ge(self.parted[s], NCH * it + c + 1)
                for j, part in enumerate(order):
                    dst = self.scr[s][j * HD:(j + 1) * HD, :, bass.ds((it * NCH + c) * CH, CH)]
                    sp.dma_start(dst.rearrange("d h t -> (d h) t"), self.part[s][:, c, part, :])\
                        .then_inc(self.written[c], 16)

    def end(self, sp):
        for c in range(NCH):
            sp.wait_ge(self.written[c], 2 * NPROD * 16 * NLOOP)


def rows(t):
    return t.rearrange("p (t f) -> p t f", f=P)


def banks(ps):
    return [ps[:, n * BANK:(n + 1) * BANK] for n in range(8)]


def first_stage(nc, taken, W, C, R, scr_q, scr_k, x_tm, v_tm, ident, roots):
    with ExitStack() as ctx:
        def sb(n, shape=(P, NCH, CH), dt=F32):
            return ctx.enter_context(nc.sbuf_tensor(f"a_{n}", list(shape), dt))

        sem = stage_semaphores(nc, ctx, "a", taken)

        n_tm, xT, q32, k32 = sb("n_tm"), sb("xT"), sb("q32"), sb("k32")
        bank = banks(ctx.enter_context(nc.psum_tensor("a_ps", [P, 8 * BANK], F32)))
        ln = Norm(ctx, nc, taken, "a_ln", roots)
        qkv = Qkv(ctx, nc, taken, "a_qkv", W("q0"), W("k0"), W("v0"), C("bq0"), C("bk0"), R("bv0"),
                  scr_q, scr_k, v_tm, (q32, k32))
        n_turned, x_ready = sem("n_turned"), sem("x_ready")
        block = ctx.enter_context(nc.Block())

        @block.sync
        def _(sp):
            with sp.Fori(0, NLOOP) as it:
                qkv.write(sp, it)
            qkv.end(sp)

        @block.gpsimd
        def _(pool):
            with pool.Fori(0, NLOOP) as it:
                for c in range(NCH):
                    ln.root(pool, NCH * it + c, c)
                qkv.rest(pool, 1, it)

        @block.scalar
        def _(act):
            with act.Fori(0, NLOOP) as it:
                for c in range(NCH):
                    act.wait_ge(n_turned, NCH * it + c + 1)
                    act.activation(xT[:, c, :], bank[c], ACT.Identity, bias=C("b_attn"), scale=C("g_attn"))\
                        .then_inc(x_ready, 1)
                qkv.act(act, it, bank)

        @block.vector
        def _(dve):
            with dve.Fori(0, NLOOP) as it:
                ln.on_vector(dve, NCH * it, lambda c: None, lambda c: x_tm[:, chunk_tiles(it, c), :],
                             lambda c: rows(n_tm[:, c, :]))
                qkv.values(dve, it, bank)
                qkv.rest(dve, 0, it)

        @block.tensor
        def _(pe):
            with pe.Fori(0, NLOOP) as it:
                for c in range(NCH):
                    pe.wait_ge(ln.done, NCH * it + c + 1)
                    pe.wait_ge(qkv.ev[1], NCH * it)
                    turn(pe, bank[c], n_tm[:, c, :], ident).then_inc(n_turned, 1)
                qkv.pe(pe, it, x_ready, xT, bank)


def middle_stage(nc, taken, W, C, R, scr_q, scr_k, x_tm, v_tm, attn_tm, ident, roots, wx_step, w_lin):
    with ExitStack() as ctx:
        def sb(n, shape=(P, NCH, CH), dt=F32):
            return ctx.enter_context(nc.sbuf_tensor(f"m_{n}", list(shape), dt))

        sem = stage_semaphores(nc, ctx, "m", taken)

        at = u = sb("at_u")
        aT = t = sb("aT_t")
        cT = hT = sb("cT_hT")
        x1 = x3 = sb("x1_x3")
        n_tm = sb("n_tm")
        xs = y1 = sb("xs_y1")
        w = y2 = sb("w_y2")
        x2 = y2p = sb("x2_y2p")
        xx = sb("xx")
        hh = [sb(f"hh{i}", (P, 4, CH)) for i in range(2)]
        bank = banks(ctx.enter_context(nc.psum_tensor("m_ps", [P, 8 * BANK], F32)))
        ln1, ln2, ln3, ln4 = (Norm(ctx, nc, taken, f"m_ln{i}", roots) for i in range(1, 5))
        qkv = Qkv(ctx, nc, taken, "m_qkv", W("q1"), W("k1"), W("v1"), C("bq1"), C("bk1"), R("bv1"),
                  scr_q, scr_k, v_tm, (hh[0], hh[1]))
        (at_ready, at_turned, aT_ready, c_mm, cT_ready, c_turned, x1_ready, n1_turned, xs_ready, z_ready,
         tanhed, lagged, sped, moved, xs_turned, xb_ready, x2_ready, xx_ready, n2_turned, hT_ready, f_mm, gelued,
         o_mm, x3_ready, y1_turned, y1T_ready, lin_mm, y2p_ready, y2_turned, y2T_ready, y2_kept) = (sem(n) for n in (
             "at_ready at_turned aT_ready c_mm cT_ready c_turned x1_ready n1_turned xs_ready z_ready tanhed lagged "
             "sped moved xs_turned xb_ready x2_ready xx_ready n2_turned hT_ready f_mm gelued o_mm x3_ready y1_turned "
             "y1T_ready lin_mm y2p_ready y2_turned y2T_ready y2_kept").split())
        block = ctx.enter_context(nc.Block())

        @block.sync
        def _(sp):
            with sp.Fori(0, NLOOP) as it:
                qkv.write(sp, it)
            qkv.end(sp)

        @block.gpsimd
        def _(pool):
            with pool.Fori(0, NLOOP) as it:
                n0 = NCH * it
                for c in range(NCH):
                    ln1.root(pool, n0 + c, c)
                for c in range(NCH):
                    pool.tensor_tensor(rows(xx[:, c, :]), x_tm[:, chunk_tiles(it, c), :],
                                       R("fb2").unsqueeze(1).to_broadcast([P, CT, P]), ALU.add)\
                        .then_inc(xb_ready, 1)
                for k in range(ITERS):
                    for c in range(NCH):
                        m = (ITERS * it + k) * NCH + c
                        pool.wait_ge(tanhed, m + 1)
                        if k:
                            pool.wait_ge(moved, m - NCH + 1)
                        pool.tensor_tensor((t if k else w)[:, c, :], u[:, c, :], xs[:, c, :], ALU.subtract)\
                            .then_inc(lagged, 1)
                for c in range(NCH):
                    pool.wait_ge(x2_ready, n0 + c + 1)
                    pool.wait_ge(xb_ready, n0 + c + 1)
                    pool.tensor_tensor(xx[:, c, :], xx[:, c, :], x2[:, c, :], ALU.add).then_inc(xx_ready, 1)
                for c in range(NCH):
                    ln2.root(pool, n0 + c, c)
                for c in range(NCH):
                    ln3.root(pool, n0 + c, c)
                for c in range(NCH):
                    ln4.root(pool, n0 + c, c)
                qkv.rest(pool, 1, it)

        @block.scalar
        def _(act):
            with act.Fori(0, NLOOP) as it:
                n0 = NCH * it
                for c in range(NCH):
                    act.activation(rows(at[:, c, :]), attn_tm[:, chunk_tiles(it, c), :], ACT.Copy)\
                        .then_inc(at_ready, 1)
                for c in range(NCH):
                    act.wait_ge(at_turned, n0 + c + 1)
                    act.activation(aT[:, c, :], bank[c], ACT.Copy).then_inc(aT_ready, 1)
                for c in range(NCH):
                    act.wait_ge(c_mm, n0 + c + 1)
                    act.activation(cT[:, c, :], bank[4 + c], ACT.Identity, bias=C("bo0")).then_inc(cT_ready, 1)
                for c in range(NCH):
                    act.wait_ge(n1_turned, n0 + c + 1)
                    act.activation(xs[:, c, :], bank[4 + c], ACT.Identity, bias=C("b1"), scale=C("g1"))\
                        .then_inc(xs_ready, 1)
                for k in range(ITERS):
                    for c in range(NCH):
                        m = (ITERS * it + k) * NCH + c
                        act.wait_ge(z_ready, m + 1)
                        act.activation(u[:, c, :], bank[c], ACT.Tanh, bias=C("b_inl")).then_inc(tanhed, 1)
                for c in range(NCH):
                    act.wait_ge(n2_turned, n0 + c + 1)
                    act.activation(hT[:, c, :], bank[c], ACT.Identity, bias=C("b2"), scale=C("g2"))\
                        .then_inc(hT_ready, 1)
                for c in range(NCH):
                    for j in range(4):
                        act.wait_ge(f_mm, 4 * (n0 + c) + j + 1)
                        if c >= 2:
                            act.wait_ge(o_mm, n0 + c - 1)
                        act.activation(hh[c % 2][:, j, :], bank[4 + j], ACT.Gelu, bias=C(f"f{j}"))\
                            .then_inc(gelued, 1)
                for c in range(NCH):
                    act.wait_ge(y1_turned, n0 + c + 1)
                    act.activation(hT[:, c, :], bank[4 + c], ACT.Copy).then_inc(y1T_ready, 1)
                for c in range(NCH):
                    act.wait_ge(y2_turned, n0 + c + 1)
                    act.activation(hT[:, c, :], bank[4 + c], ACT.Copy).then_inc(y2T_ready, 1)
                    act.activation(x_tm[:, chunk_tiles(it, c), :], rows(y2[:, c, :]), ACT.Copy).then_inc(y2_kept, 1)
                qkv.act(act, it, bank)

        @block.vector
        def _(dve):
            def norm(ln, n0, before, src, dst):
                ln.on_vector(dve, n0, before, lambda c: rows(src[:, c, :]), lambda c: rows(dst[:, c, :]))

            with dve.Fori(0, NLOOP) as it:
                n0 = NCH * it
                def before_ln1(c):
                    dve.wait_ge(c_turned, n0 + c + 1)
                    dve.tensor_tensor(rows(x1[:, c, :]), rows(bank[c]), x_tm[:, chunk_tiles(it, c), :], ALU.add)\
                        .then_inc(x1_ready, 1)
                    dve.wait_ge(x1_ready, n0 + c + 1)

                norm(ln1, n0, before_ln1, x1, n_tm)
                for k in range(ITERS):
                    for c in range(NCH):
                        m = (ITERS * it + k) * NCH + c
                        dve.wait_ge(lagged, m + 1)
                        if k:
                            dve.scalar_tensor_tensor(out=w[:, c, :], in0=w[:, c, :], scalar=1.0 - DT, in1=t[:, c, :],
                                                     op0=ALU.mult, op1=ALU.add).then_inc(sped, 1)
                            dve.wait_ge(sped, ((ITERS - 1) * it + k - 1) * NCH + c + 1)
                        dve.scalar_tensor_tensor(out=xs[:, c, :], in0=w[:, c, :], scalar=DT * DT, in1=xs[:, c, :],
                                                 op0=ALU.mult, op1=ALU.add).then_inc(moved, 1)
                def before_ln2(c):
                    dve.wait_ge(xs_turned, n0 + c + 1)
                    dve.tensor_tensor(x2[:, c, :], bank[4 + c], x1[:, c, :], ALU.add).then_inc(x2_ready, 1)
                    dve.wait_ge(x2_ready, n0 + c + 1)

                norm(ln2, n0, before_ln2, x2, n_tm)
                def before_ln3(c):
                    dve.wait_ge(o_mm, n0 + c + 1)
                    dve.wait_ge(xx_ready, n0 + c + 1)
                    dve.tensor_tensor(x3[:, c, :], bank[c], xx[:, c, :], ALU.add).then_inc(x3_ready, 1)
                    dve.wait_ge(x3_ready, n0 + c + 1)

                norm(ln3, n0, before_ln3, x3, y1)
                def before_ln4(c):
                    dve.wait_ge(lin_mm, n0 + c + 1)
                    dve.tensor_tensor(y2p[:, c, :], bank[c], y1[:, c, :], ALU.add).then_inc(y2p_ready, 1)
                    dve.wait_ge(y2p_ready, n0 + c + 1)

                norm(ln4, n0, before_ln4, y2p, y2)
                qkv.values(dve, it, bank)
                qkv.rest(dve, 0, it)

        @block.tensor
        def _(pe):
            with pe.Fori(0, NLOOP) as it:
                n0 = NCH * it
                for c in range(NCH):
                    pe.wait_ge(at_ready, n0 + c + 1)
                    pe.wait_ge(qkv.ev[1], n0)
                    turn(pe, bank[c], at[:, c, :], ident).then_inc(at_turned, 1)
                for c in range(NCH):
                    pe.wait_ge(aT_ready, n0 + c + 1)
                    pe.wait_ge(qkv.v_ev, n0)
                    pe.matmul(bank[4 + c], W("o0"), aT[:, c, :], start=True, stop=True).then_inc(c_mm, 1)
                for c in range(NCH):
                    pe.wait_ge(cT_ready, n0 + c + 1)
                    turn(pe, bank[c], cT[:, c, :], ident).then_inc(c_turned, 1)
                for c in range(NCH):
                    pe.wait_ge(ln1.done, n0 + c + 1)
                    turn(pe, bank[4 + c], n_tm[:, c, :], ident).then_inc(n1_turned, 1)
                for c in range(NCH):
                    pe.wait_ge(xs_ready, n0 + c + 1)
                    pe.matmul(bank[c], W("ctx"), cT[:, c, :], start=True, stop=False)
                    pe.matmul(bank[c], W("x"), xs[:, c, :], start=False, stop=True).then_inc(z_ready, 1)
                for k in range(ITERS - 1):
                    for c in range(NCH):
                        if k:
                            pe.wait_ge(sped, ((ITERS - 1) * it + k - 1) * NCH + c + 1)
                        else:
                            pe.wait_ge(lagged, ITERS * n0 + c + 1)
                        pe.matmul(bank[c], wx_step, w[:, c, :], start=False, stop=True, skip_group_check=True)\
                            .then_inc(z_ready, 1)
                for c in range(NCH):
                    pe.wait_ge(moved, (ITERS * it + ITERS - 1) * NCH + c + 1)
                    turn(pe, bank[4 + c], xs[:, c, :], ident).then_inc(xs_turned, 1)
                for c in range(NCH):
                    pe.wait_ge(ln2.done, n0 + c + 1)
                    turn(pe, bank[c], n_tm[:, c, :], ident).then_inc(n2_turned, 1)

                def down(c):
                    pe.wait_ge(gelued, 4 * (n0 + c) + 4)
                    for i in range(CT):
                        for j in range(4):
                            last = pe.matmul(bank[c][:, i * P:(i + 1) * P], hh[c % 2][:, j, i * P:(i + 1) * P],
                                             W("f2")[:, j * P:(j + 1) * P], start=j == 0, stop=j == 3)
                    last.then_inc(o_mm, 1)

                pe.wait_ge(x2_ready, n0 + NCH)
                for c in range(NCH):
                    pe.wait_ge(hT_ready, n0 + c + 1)
                    for j in range(4):
                        if c:
                            pe.wait_ge(gelued, 4 * (n0 + c - 1) + j + 1)
                        pe.matmul(bank[4 + j], W("f1")[:, j * P:(j + 1) * P], hT[:, c, :], start=True, stop=True)\
                            .then_inc(f_mm, 1)
                    if c:
                        down(c - 1)
                down(NCH - 1)
                for c in range(NCH):
                    pe.wait_ge(ln3.done, n0 + c + 1)
                    turn(pe, bank[4 + c], y1[:, c, :], ident).then_inc(y1_turned, 1)
                for c in range(NCH):
                    pe.wait_ge(y1T_ready, n0 + c + 1)
                    tokens_out(pe, bank[c], hT[:, c, :], w_lin).then_inc(lin_mm, 1)
                for c in range(NCH):
                    pe.wait_ge(ln4.done, n0 + c + 1)
                    turn(pe, bank[4 + c], y2[:, c, :], ident).then_inc(y2_turned, 1)
                qkv.pe(pe, it, y2T_ready, hT, bank)


def last_stage(nc, taken, W, C, R, out, x_tm, attn_tm, ident, roots):
    with ExitStack() as ctx:
        def sb(n, shape=(P, NCH, CH), dt=F32):
            return ctx.enter_context(nc.sbuf_tensor(f"e_{n}", list(shape), dt))

        sem = stage_semaphores(nc, ctx, "e", taken)

        at, aT, xb, x1, y3, yb, hT, x4, y4 = (sb(n) for n in "at aT xb x1 y3 yb hT x4 y4".split())
        hh = [sb(f"hh{i}", (P, 4, CH)) for i in range(2)]
        bank = banks(ctx.enter_context(nc.psum_tensor("e_ps", [P, 8 * BANK], F32)))
        ln5, ln6 = (Norm(ctx, nc, taken, f"e_ln{i}", roots) for i in (5, 6))
        (at_ready, at_turned, aT_ready, o_mm, xb_ready, x1_ready, yb_ready, y3_turned, hT_ready, f_mm, relued, d_mm,
         x4_ready) = (sem(n) for n in ("at_ready at_turned aT_ready o_mm xb_ready x1_ready yb_ready y3_turned "
                                       "hT_ready f_mm relued d_mm x4_ready").split())
        stored = [sem(f"stored{c}") for c in range(NCH)]
        block = ctx.enter_context(nc.Block())

        @block.sync
        def _(sp):
            with sp.Fori(0, NLOOP) as it:
                for c in range(NCH):
                    sp.wait_ge(ln6.done, NCH * it + c + 1)
                    sp.dma_start(out.rearrange("b (n p) d -> p (b n) d", p=P)[:, chunk_tiles(it, c), :],
                                 rows(y4[:, c, :])).then_inc(stored[c], 16)
            for c in range(NCH):
                sp.wait_ge(stored[c], 16 * NLOOP)

        @block.gpsimd
        def _(pool):
            with pool.Fori(0, NLOOP) as it:
                n0 = NCH * it
                for c in range(NCH):
                    pool.tensor_tensor(rows(xb[:, c, :]), x_tm[:, chunk_tiles(it, c), :],
                                       R("bo1").unsqueeze(1).to_broadcast([P, CT, P]), ALU.add)\
                        .then_inc(xb_ready, 1)
                for c in range(NCH):
                    ln5.root(pool, n0 + c, c)
                for c in range(NCH):
                    pool.wait_ge(ln5.done, n0 + c + 1)
                    pool.tensor_tensor(rows(yb[:, c, :]), rows(y3[:, c, :]),
                                       R("hb2").unsqueeze(1).to_broadcast([P, CT, P]), ALU.add)\
                        .then_inc(yb_ready, 1)
                for c in range(NCH):
                    ln6.root(pool, n0 + c, c)

        @block.scalar
        def _(act):
            with act.Fori(0, NLOOP) as it:
                n0 = NCH * it
                for c in range(NCH):
                    act.activation(rows(at[:, c, :]), attn_tm[:, chunk_tiles(it, c), :], ACT.Copy)\
                        .then_inc(at_ready, 1)
                for c in range(NCH):
                    act.wait_ge(at_turned, n0 + c + 1)
                    act.activation(aT[:, c, :], bank[c], ACT.Copy).then_inc(aT_ready, 1)
                for c in range(NCH):
                    act.wait_ge(y3_turned, n0 + c + 1)
                    act.activation(hT[:, c, :], bank[c], ACT.Copy).then_inc(hT_ready, 1)
                for c in range(NCH):
                    for j in range(4):
                        act.wait_ge(f_mm, 4 * (n0 + c) + j + 1)
                        if c >= 2:
                            act.wait_ge(d_mm, n0 + c - 1)
                        act.activation(hh[c % 2][:, j, :], bank[4 + j], ACT.Relu, bias=C(f"h{j}"))\
                            .then_inc(relued, 1)

        @block.vector
        def _(dve):
            def norm(ln, n0, before, src, dst):
                ln.on_vector(dve, n0, before, lambda c: rows(src[:, c, :]), lambda c: rows(dst[:, c, :]))

            with dve.Fori(0, NLOOP) as it:
                n0 = NCH * it

                def before_ln5(c):
                    dve.wait_ge(o_mm, n0 + c + 1)
                    dve.wait_ge(xb_ready, n0 + c + 1)
                    dve.tensor_tensor(x1[:, c, :], bank[4 + c], xb[:, c, :], ALU.add).then_inc(x1_ready, 1)
                    dve.wait_ge(x1_ready, n0 + c + 1)

                norm(ln5, n0, before_ln5, x1, y3)

                def before_ln6(c):
                    dve.wait_ge(d_mm, n0 + c + 1)
                    dve.wait_ge(yb_ready, n0 + c + 1)
                    dve.tensor_tensor(x4[:, c, :], bank[c], yb[:, c, :], ALU.add).then_inc(x4_ready, 1)
                    dve.wait_ge(x4_ready, n0 + c + 1)

                for c in range(NCH):
                    dve.wait_ge(stored[c], 16 * it)
                norm(ln6, n0, before_ln6, x4, y4)

        @block.tensor
        def _(pe):
            with pe.Fori(0, NLOOP) as it:
                n0 = NCH * it
                for c in range(NCH):
                    pe.wait_ge(at_ready, n0 + c + 1)
                    pe.wait_ge(x4_ready, n0)
                    turn(pe, bank[c], at[:, c, :], ident).then_inc(at_turned, 1)
                for c in range(NCH):
                    pe.wait_ge(aT_ready, n0 + c + 1)
                    pe.wait_ge(relued, 4 * n0)
                    tokens_out(pe, bank[4 + c], aT[:, c, :], W("o1")).then_inc(o_mm, 1)
                for c in range(NCH):
                    pe.wait_ge(ln5.done, n0 + c + 1)
                    turn(pe, bank[c], y3[:, c, :], ident).then_inc(y3_turned, 1)

                def down(c):
                    pe.wait_ge(relued, 4 * (n0 + c) + 4)
                    for i in range(CT):
                        for j in range(4):
                            last = pe.matmul(bank[c][:, i * P:(i + 1) * P], hh[c % 2][:, j, i * P:(i + 1) * P],
                                             W("g2")[:, j * P:(j + 1) * P], start=j == 0, stop=j == 3)
                    last.then_inc(d_mm, 1)

                pe.wait_ge(x1_ready, n0 + NCH)
                for c in range(NCH):
                    pe.wait_ge(hT_ready, n0 + c + 1)
                    for j in range(4):
                        if c:
                            pe.wait_ge(relued, 4 * (n0 + c - 1) + j + 1)
                        pe.matmul(bank[4 + j], W("g1")[:, j * P:(j + 1) * P], hT[:, c, :], start=True, stop=True)\
                            .then_inc(f_mm, 1)
                    if c:
                        down(c - 1)
                down(NCH - 1)


def two_layer_kernel(nc, x, w_pack, c_pack, r_pack, out):
    scr = [nc.dram_tensor(f"scr_{n}", [ROWS, H, TOK], BF16, kind="Internal").ap() for n in ("q0", "k0", "q1", "k1")]
    scr_m = [nc.dram_tensor(f"scr_m{i}", [3, B * H * QT, P], BF16, kind="Internal").ap() for i in range(2)]
    with ExitStack() as ctx:
        def sb(n, shape, dt=F32):
            return ctx.enter_context(nc.sbuf_tensor(n, shape, dt))

        def sem(n):
            return ctx.enter_context(nc.semaphore(n))

        x_tm = sb("x_tm", [P, TILES, D])
        v_tm = sb("v_tm", [P, TILES, D])
        attn_tm = sb("attn_tm", [P, TILES, D])
        w_sb = sb("w_sb", [P, W_COLS])
        c_sb = sb("c_sb", [P, len(C_AT)])
        r_sb = sb("r_sb", [P, len(R_AT), D])
        wx_step = sb("wx_step", [P, D])
        w_lin = sb("w_lin", [P, D])
        ident = sb("ident", [P, P])
        ident_bf = sb("ident_bf", [P, P], BF16)
        mask_neg = sb("mask_neg", [P, P], BF16)
        roots = [sb("eps", [P, CT]), sb("neg_half", [P, CT])]

        def W(n):
            at, width = W_AT[n]
            return w_sb[:, at:at + width]

        def C(n):
            return c_sb[:, C_AT[n]:C_AT[n] + 1]

        def R(n):
            return r_sb[:, R_AT[n], :]

        x_in, w_in, small_in, blank, cut_out = (sem(n) for n in "x_in w_in small_in blank cut_out".split())
        with nc.Block() as block:
            @block.sync
            def _(sp):
                sp.dma_start(c_sb[:, :], c_pack).then_inc(small_in, 16)
                sp.dma_start(r_sb[:, :, :], r_pack.unsqueeze(0).to_broadcast([P, len(R_AT), D])).then_inc(small_in, 16)
                for b in range(B):
                    sp.dma_start(x_tm[:, b * QT:(b + 1) * QT, :],
                                 x[b, :, :].rearrange("(n p) d -> p n d", p=P)).then_inc(x_in, 16)
                sp.wait_ge(small_in, 32)
                sp.wait_ge(x_in, 16 * B)

            @block.scalar
            def _(act):
                act.dma_start(w_sb[:, :], w_pack).then_inc(w_in, 16)

            @block.gpsimd
            def _(pool):
                pool.memset(ident[:, :], 0.0).then_inc(blank, 1)
                pool.memset(mask_neg[:, :], 0.0).then_inc(blank, 1)
                pool.memset(roots[0][:, :], EPS)
                pool.memset(roots[1][:, :], -0.5)
                pool.wait_ge(blank, 2)
                pool.affine_select(out=ident[:, :], in_=ident[:, :], compare_op=ALU.not_equal, fill=1.0, base=0,
                                   pattern=[[-1, P]], channel_multiplier=1).then_inc(cut_out, 1)
                pool.affine_select(out=mask_neg[:, :], in_=mask_neg[:, :], compare_op=ALU.is_ge, fill=-3.0e38, base=0,
                                   pattern=[[-1, P]], channel_multiplier=1).then_inc(cut_out, 1)

            @block.vector
            def _(dve):
                dve.wait_ge(cut_out, 1)
                dve.tensor_copy(ident_bf[:, :], ident[:, :])
                dve.wait_ge(w_in, 16)
                dve.tensor_scalar(wx_step[:, :], W("x"), DT * DT, None, ALU.mult)
                dve.tensor_tensor(w_lin[:, :], W("lin"), W("dis"), ALU.add)

        taken = []
        first_stage(nc, taken, W, C, R, scr[0], scr[1], x_tm, v_tm, ident[:, :], roots)
        attention(nc, taken, "l0", True, scr[0], scr[1], scr_m[0], v_tm, attn_tm, ident[:, :], mask_neg[:, :],
                  ident_bf[:, :])
        retire(nc, taken)
        middle_stage(nc, [], W, C, R, scr[2], scr[3], x_tm, v_tm, attn_tm, ident[:, :], roots, wx_step[:, :],
                     w_lin[:, :])
        attention(nc, [], "l1", False, scr[2], scr[3], scr_m[1], v_tm, attn_tm, ident[:, :], mask_neg[:, :],
                  ident_bf[:, :])
        last_stage(nc, [], W, C, R, out, x_tm, attn_tm, ident[:, :], roots)


def kernel(**inputs):
    import numpy as np
    import concourse.bacc as bacc
    from concourse import mybir as mb
    from concourse.bass_utils import run_bass_kernel_spmd

    a = {n: np.asarray(v) for n, v in inputs.items()}

    def by_dim(w):
        return w.reshape(w.shape[:-1] + (H, HD)).swapaxes(-1, -2).reshape(w.shape)

    def parts0(w):
        q, k, v = (w[..., n * D:(n + 1) * D] for n in range(3))
        return by_dim(q), by_dim(k), v

    def parts1(w):
        w = w.reshape(w.shape[:-1] + (H, 3, HD))
        q, k, v = (w[..., n, :].reshape(w.shape[:-3] + (D,)) for n in range(3))
        return by_dim(q), by_dim(k), v

    def by_rows(w):
        return w.reshape(4, P, D).transpose(1, 0, 2).reshape(P, 4 * D)

    disha = a["L0_ffn_disha"]
    w_pack = np.concatenate([
        *parts0(a["L0_attn_qkv_w"]), a["L0_attn_out_w"], a["L0_attn_w_ctx"], a["L0_attn_w_x"], a["L0_attn_ff_w1"],
        by_rows(a["L0_attn_ff_w2"]), a["L0_ffn_weight"].T, np.concatenate([disha, disha], axis=0),
        *parts1(a["L1_attn_Wqkv"]), a["L1_attn_Wout"], a["L1_ffn_W1"], by_rows(a["L1_ffn_W2"])], axis=1)
    bq0, bk0, bv0 = parts0(a["L0_attn_qkv_b"])
    bq1, bk1, bv1 = parts1(a["L1_attn_bqkv"])
    c_pack = np.stack([
        bq0, bk0, a["L0_attn_out_b"], a["L0_attn_g_attn"], a["L0_attn_b_attn"], a["L0_attn_g1"], a["L0_attn_b1"],
        a["L0_attn_g2"], a["L0_attn_b2"], a["L0_attn_b_inl"], *a["L0_attn_ff_b1"].reshape(4, P),
        bq1, bk1, *a["L1_ffn_b1"].reshape(4, P)], axis=1)
    r_pack = np.stack([bv0, a["L0_attn_ff_b2"], bv1, a["L1_attn_bout"], a["L1_ffn_b2"]])

    nc = bacc.Bacc("TRN2", target_bir_lowering=False, num_devices=1)
    arrays, args = {}, []
    for name, v in (("x", a["L0_attn_x"]), ("w_pack", w_pack), ("c_pack", c_pack), ("r_pack", r_pack)):
        v = np.ascontiguousarray(v)
        arrays[f"in_{name}"] = v
        args.append(nc.dram_tensor(f"in_{name}", v.shape, mb.dt.from_np(v.dtype), kind="ExternalInput").ap())
    args.append(nc.dram_tensor("out_0", (B, SEQ, D), mb.dt.float32, kind="ExternalOutput").ap())
    two_layer_kernel(nc, *args)
    r = run_bass_kernel_spmd(nc, [arrays], core_ids=[0])
    return r.results[0]["out_0"]
```

```python
import concourse.bass as bass
from concourse import mybir
from contextlib import ExitStack

F32 = mybir.dt.float32
BF16 = mybir.dt.bfloat16
ALU = mybir.AluOpType
ACT = mybir.ActivationFunctionType
AX_X = mybir.AxisListType.X

P = 128
B, SEQ, D = 4, 1024, 128
H, HD = 16, 8
FF = 512
ITERS = 8
DT = 0.1
EPS = 1e-5
TOK = B * SEQ
TILES = TOK // P
BANK = 512
CH = 512
CT = CH // P
NCH = 4
NLOOP = TOK // (CH * NCH)

QPART = (0, 0, 0, 1, 1, 2)
KPART = (0, 1, 2, 0, 1, 0)
NPROD = len(QPART)
ROWS = NPROD * HD
MROW = 96
GH = 4
NG = H // GH
QT = SEQ // P
QH = SEQ // CH
SCALE = 1.0 / float(HD) ** 0.5

W_AT = {}
_at = 0
for _n, _w in (("q0", D), ("k0", D), ("v0", D), ("o0", D), ("ctx", D), ("x", D), ("f1", FF), ("f2", FF),
               ("lin", D), ("dis", D), ("q1", D), ("k1", D), ("v1", D), ("o1", D), ("g1", FF), ("g2", FF)):
    W_AT[_n] = (_at, _w)
    _at += _w
W_COLS = _at
C_AT = {n: i for i, n in enumerate(
    ("bq0", "bk0", "bo0", "g_attn", "b_attn", "g1", "b1", "g2", "b2", "b_inl", "f0", "f1", "f2", "f3",
     "bq1", "bk1", "h0", "h1", "h2", "h3"))}
R_AT = {n: i for i, n in enumerate(("bv0", "fb2", "bv1", "bo1", "hb2"))}


def chunk_tiles(it, c):
    return bass.ds((it * NCH + c) * CT, CT)


def attention_steps(causal):
    return [(qh, kt, max(0, kt * P - qh * CH) if causal else 0) for qh in range(QH) for kt in range(QT)
            if not causal or kt * P < (qh + 1) * CH]


def score_units(causal):
    out = []
    for h in range(GH):
        for qt in range(QT):
            keys = (qt + 1) * P if causal else SEQ
            out += [(h, qt, n, at, min(BANK, keys - at)) for n, at in enumerate(range(0, keys, BANK))]
    return out



def stage_semaphores(nc, ctx, prefix, taken):
    def sem(n):
        taken.append(ctx.enter_context(nc.semaphore(f"{prefix}_{n}")))
        return taken[-1]
    return sem


def retire(nc, taken):
    with nc.Block() as block:
        @block.sync
        def _(sp):
            for s in taken:
                sp.sem_clear(s)


def attention(nc, taken, name, causal, scr_q, scr_k, scr_m, v_tm, attn_tm, ident, mask_neg, ident_bf):
    steps = attention_steps(causal)
    units = score_units(causal)
    NS, NU = len(steps), len(units)
    first_of = [min(n for n, s in enumerate(steps) if s[0] == qh) for qh in range(QH)]
    last_of = [max(n for n, s in enumerate(steps) if s[0] == qh) for qh in range(QH)]
    heads_of = [((0, 1, 2, 3),) if CH - lo <= BANK // 2 else ((0, 1), (2, 3)) for _, _, lo in steps]
    exp_before = [sum(len(x) for x in heads_of[:n]) for n in range(NS + 1)]
    NE = exp_before[NS]
    diagonal = [causal and kt * P >= qh * CH for qh, kt, _ in steps]
    ND = sum(diagonal)
    PRING = 4
    assert NE % 2 == 0 and NU % 2 == 0 and (NG * NS) % PRING == 0
    LOADS = 2 * 16
    LEAD = NU // 3 // 2 * 2

    stream = [(1 + (LEAD + i) // NU, (LEAD + i) % NU) for i in range(NG * NU)]
    cost = [CH - steps[m % NS][2] for m in range(NG * NS)]
    weight = [units[k][4] + 64 for _, k in stream]
    beside, at = [], 0
    for m in range(NG * NS):
        upto = at
        while upto < len(stream) and (sum(weight[:upto]) + weight[upto] / 2) / sum(weight) < sum(cost[:m + 1]) / sum(cost):
            upto += 1
        if m == NG * NS - 1:
            upto = len(stream)
        beside.append(stream[at:upto])
        at = upto
    through = [[] for _ in range(NG * NS + 2)]
    for u in range(NG):
        for qh in range(QH):
            through[u * NS + last_of[qh] + 2].append(("out", u, qh))
    for m in range(NG * NS):
        for r, k in beside[m]:
            if k == NU - 1:
                at = m + 1
                while through[at]:
                    at += 1
                through[at].append(("max", r))

    def batch_schedule(last):
        keep = (lambda r: r < NG) if last else (lambda r: True)
        return ([[x for x in b if keep(x[0])] for b in beside],
                [[x for x in t if x[0] == "out" or keep(x[1])] for t in through])

    TURNS = sum(len(t) for t in through)
    FREE = 1

    with ExitStack() as ctx:
        def sb(n, shape, dt):
            return ctx.enter_context(nc.sbuf_tensor(f"{name}_{n}", shape, dt))

        sem = stage_semaphores(nc, ctx, name, taken)
        Qs = [sb(f"Qs{i}", [P, GH, SEQ], BF16) for i in range(NG)]
        Ks = [sb(f"Ks{i}", [P, GH, SEQ], BF16) for i in range(NG)]
        pT = [sb(f"pT{i}", [P, GH, CH], F32) for i in range(PRING)]
        vs = [sb(f"vs{i}", [P, QT, GH, 32], F32) for i in range(2)]
        negp = [sb(f"negp{i}", [P, GH * QT, 2], F32) for i in range(2)]
        negm = sb("negm", [P, GH * QT], F32)
        msp = sb("msp", [GH * QT, 3, P], BF16)
        mres = sb("mres", [GH * QT, 2, P], F32)
        outT = sb("outT", [P, CH], F32)
        rc = sb("rc", [P, CT, GH], F32)
        held = sb("held", [P, 2], F32)
        ps = ctx.enter_context(nc.psum_tensor(f"{name}_ps", [P, 8 * BANK], F32))
        s_ps = [ps[:, n * BANK:(n + 1) * BANK] for n in range(2)]
        st_ps = [ps[:, (2 + 2 * n) * BANK:(4 + 2 * n) * BANK] for n in range(2)]
        pv_ps = ps[:, 6 * BANK:7 * BANK]
        t_ps = ps[:, 7 * BANK:8 * BANK]

        cleared = [sem(f"cleared{i}") for i in range(NG)]
        ones_set = sem("ones_set")
        negp_set = sem("negp_set")
        loaded = [sem(f"loaded{i}") for i in range(NG)]
        max_rows = [sem(f"max_rows{i}") for i in range(NG)]
        scored = sem("scored")
        reduced = sem("reduced")
        keyed = sem("keyed")
        exped = sem("exped")
        masked = sem("masked")
        weighed = sem("weighed")
        evacuated = sem("evacuated")
        turned = sem("turned")
        recips = sem("recips")
        turn_read = sem("turn_read")
        max_joined = sem("max_joined")
        max_turned = sem("max_turned")
        max_part = sem("max_part")
        max_split = sem("max_split")
        max_stored = sem("max_stored")
        v_clear = sem("v_clear")
        v_ready = sem("v_ready")
        block = ctx.enter_context(nc.Block())

        def clear(eng, slots):
            for u in slots:
                for t in (Qs[u], Ks[u]):
                    eng.memset(t[:, :, :].rearrange("p h t -> p (h t)").bitcast(F32), 0.0).then_inc(cleared[u], 1)

        @block.sync
        def _(sp):
            def load(b, u):
                for scr, slot in ((scr_q, Qs[u]), (scr_k, Ks[u])):
                    sp.dma_start(slot[0:ROWS, :, :],
                                 scr[:, u * GH:(u + 1) * GH, bass.ds(b * SEQ, SEQ)]).then_inc(loaded[u], 16)

            def put_max(g, u):
                sp.wait_ge(max_split, g + 1)
                mine = scr_m[:, bass.ds(g * GH * QT, GH * QT), :]
                sp.dma_start(mine.rearrange("s r c -> r s c"), msp[:, :, :]).then_inc(max_stored, 16)
                sp.wait_ge(max_stored, 16 * (g + 1))
                sp.dma_start(Qs[u][MROW:MROW + 3, :, :].rearrange("p h (t c) -> p (h t) c", c=P), mine)\
                    .then_inc(max_rows[u], 16)

            def body(b, u, ahead):
                g = NG * b + u
                if ahead >= 3:
                    sp.wait_ge(keyed, NE * g + 1)
                    load(b + (u + 3) // NG, (u + 3) % NG)
                if ahead >= 1:
                    put_max(g + 1, (u + 1) % NG)

            for u in range(3):
                sp.wait_ge(cleared[u], 2)
                load(0, u)
            sp.wait_ge(cleared[3], 2)
            put_max(0, 0)
            with sp.Fori(0, B - 1) as b:
                for u in range(NG):
                    body(b, u, NG)
            for u in range(NG):
                body(B - 1, u, NG - 1 - u)

        @block.gpsimd
        def _(pool):
            def values(b, u):
                pool.tensor_copy(vs[u % 2][:, :, :, 0:HD],
                                 v_tm[:, bass.ds(b * QT, QT), u * GH * HD:(u + 1) * GH * HD]
                                 .rearrange("p t (h d) -> p t h d", d=HD)).then_inc(v_ready, 1)

            def body(b, u, more):
                g = NG * b + u
                for n, (qh, kt, lo) in enumerate(steps):
                    if n == 2 and more:
                        pool.wait_ge(weighed, PRING + NS * g + 1)
                        values(b + (u + 1) // NG, (u + 1) % NG)
                    if diagonal[n]:
                        pool.wait_ge(masked, FREE + ND * g + sum(diagonal[:n]))
                        pool.wait_ge(exped, 2 * FREE + NE * g + exp_before[n + 1])
                        pool.tensor_tensor(held[:, 0:1], held[:, 1:2], held[:, 1:2], ALU.mult)
                        blk = pT[(u * NS + n) % PRING][:, :, lo:lo + P]
                        pool.affine_select(out=blk, in_=blk, compare_op=ALU.is_ge, fill=0.0, base=0,
                                           pattern=[[0, GH], [1, P]], channel_multiplier=-1)\
                            .then_inc(masked, 1)

            clear(pool, (2, 3))
            pool.memset(held[:, :], 0.0).then_inc(masked, FREE)
            for i in range(2):
                pool.memset(vs[i][:, :, :, :], 0.0).then_inc(v_clear, 1)
            pool.wait_ge(v_clear, 2)
            for i in range(2):
                pool.memset(vs[i][:, :, :, HD:HD + 1], 1.0).then_inc(v_clear, 1)
            pool.wait_ge(v_clear, 4)
            values(0, 0)
            with pool.Fori(0, B - 1) as b:
                for u in range(NG):
                    body(b, u, True)
            for u in range(NG):
                body(B - 1, u, u < NG - 1)

        @block.scalar
        def _(act):
            def evacuate(g, qh):
                act.wait_ge(weighed, PRING + NS * g + last_of[qh] + 1)
                act.wait_ge(turned, FREE + QH * g + qh)
                act.activation(outT[:, :], pv_ps, ACT.Copy).then_inc(evacuated, 1)

            with act.Fori(0, B) as b:
                due = None
                for m in range(NG * NS):
                    g, n = NG * b + m // NS, m % NS
                    qh, kt, lo = steps[n]
                    act.wait_ge(weighed, NS * NG * b + m + 1)
                    for e, hs in enumerate(heads_of[n]):
                        k = exp_before[n] + e
                        act.wait_ge(keyed, NE * g + k + 1)
                        src = st_ps[k % 2].rearrange("p (h c) -> p h c", h=len(hs))[:, :, 0:CH - lo]
                        act.activation(pT[m % PRING][:, hs[0]:hs[-1] + 1, lo:CH], src, ACT.Exp, scale=SCALE)\
                            .then_inc(exped, 1)
                    if due:
                        evacuate(*due)
                    due = (g, qh) if n == last_of[qh] else None
                evacuate(*due)

        @block.vector
        def _(dve):
            def reduce(g, r, k):
                h, qt, part, at, w = units[k]
                dve.wait_ge(scored, NU * g + k + 1)
                dve.tensor_reduce(negp[r % 2][:, h * QT + qt, part:part + 1], s_ps[k % 2][:, 0:w],
                                  AX_X, ALU.max, negate=True).then_inc(reduced, 1)
                if k == NU - 1:
                    join(g, r)

            def join(g, r):
                dve.wait_ge(reduced, NU * (g + 1))
                if not isinstance(g, int) or g:
                    dve.wait_ge(max_turned, g)
                dve.tensor_tensor(negm[:, :], negp[r % 2][:, :, 0], negp[r % 2][:, :, 1], ALU.min)\
                    .then_inc(max_joined, 1)

            def split(g, turns):
                src = t_ps[0:GH * QT, 0:P]
                dve.wait_ge(max_turned, g + 1)
                if not isinstance(g, int) or g:
                    dve.wait_ge(max_stored, 16 * g)
                dve.tensor_copy(msp[:, 0, :], src).then_inc(max_part, 1)
                dve.wait_ge(max_part, 3 * g + 1)
                dve.tensor_tensor(mres[:, 0, :], src, msp[:, 0, :], ALU.subtract).then_inc(turn_read, 1)
                dve.wait_ge(turn_read, turns + 1)
                dve.tensor_copy(msp[:, 1, :], mres[:, 0, :]).then_inc(max_part, 1)
                dve.wait_ge(max_part, 3 * g + 2)
                dve.tensor_tensor(mres[:, 1, :], mres[:, 0, :], msp[:, 1, :], ALU.subtract).then_inc(max_part, 1)
                dve.wait_ge(max_part, 3 * g + 3)
                dve.tensor_copy(msp[:, 2, :], mres[:, 1, :]).then_inc(max_split, 1)

            def norm(b, u, qh):
                half = QH * (NG * b + u) + qh
                src = t_ps.rearrange("p (t h c) -> p t h c", t=CT, h=GH)
                dve.wait_ge(turned, FREE + half + 1)
                dve.reciprocal(rc[:, :, :], src[:, :, :, HD]).then_inc(recips, 1)
                dve.wait_ge(recips, half + 1)
                dst = attn_tm[:, bass.ds(b * QT + qh * CT, CT), u * GH * HD:(u + 1) * GH * HD]
                dve.tensor_tensor(dst.rearrange("p t (h d) -> p t h d", d=HD), src[:, :, :, 0:HD],
                                  rc[:, :, :].unsqueeze(3).to_broadcast([P, CT, GH, HD]), ALU.mult)\
                    .then_inc(turn_read, 1)

            def batch(b, last):
                units_at, turns_at = batch_schedule(last)
                turns = 1 + TURNS * b
                for m in range(NG * NS + 2):
                    for what in turns_at[m - 1] if m else ():
                        if what[0] == "max":
                            split(NG * b + what[1], turns)
                        else:
                            norm(b, what[1], what[2])
                        turns = turns + 1
                    for r, k in units_at[m] if m < NG * NS else ():
                        reduce(NG * b + r, r, k)
                for what in turns_at[-1]:
                    norm(b, what[1], what[2])

            clear(dve, (0, 1))
            for u in range(NG):
                dve.wait_ge(cleared[u], 2)
                dve.memset(Ks[u][MROW:MROW + 3, :, :], 1.0).then_inc(ones_set, 1)
            dve.memset(negp[0][:, :, 1], 3.0e38).then_inc(exped, 2 * FREE)
            dve.memset(negp[1][:, :, 1], 3.0e38).then_inc(weighed, PRING)
            dve.memset(rc[:, :, :], 0.0).then_inc(evacuated, FREE)
            dve.memset(negm[:, :], 0.0).then_inc(turned, FREE)
            for started, count in ((exped, 2 * FREE), (weighed, PRING), (evacuated, FREE), (turned, FREE)):
                dve.wait_ge(started, count)
            for k in range(NU):
                reduce(0, 0, k)
            for k in range(LEAD):
                reduce(1, 1, k)
                if k == 4:
                    split(0, 0)
            with dve.Fori(0, B - 1) as b:
                batch(b, False)
            batch(B - 1, True)

        @block.tensor
        def _(pe):
            def score(g, r, k):
                h, qt, part, at, w = units[k]
                n = NU * g + k - 1
                if not isinstance(n, int) or n > 0:
                    pe.wait_ge(reduced, n)
                out = s_ps[k % 2][:, 0:w]
                s = r % NG
                diag = causal and at + w == (qt + 1) * P
                last = pe.matmul(out, Qs[s][0:MROW, h, qt * P:(qt + 1) * P], Ks[s][0:MROW, h, at:at + w],
                                 start=True, stop=True)
                if diag:
                    last = pe.matmul(out[:, w - P:w], ident_bf, mask_neg, start=False, stop=True,
                                     skip_group_check=True)
                last.then_inc(scored, 1)

            def key_scores(b, m, e):
                u, n = m // NS, m % NS
                qh, kt, lo = steps[n]
                hs, k, w = heads_of[n][e], exp_before[n] + e, CH - lo
                pe.wait_ge(exped, 2 * FREE + NE * (NG * b + u) + k - 1)
                out = st_ps[k % 2].rearrange("p (h c) -> p h c", h=len(hs))
                for i, h in enumerate(hs):
                    last = pe.matmul(out[:, i, 0:w], Ks[u][:, h, kt * P:(kt + 1) * P],
                                     Qs[u][:, h, qh * CH + lo:(qh + 1) * CH], start=True, stop=True)
                last.then_inc(keyed, 1)

            def weigh(b, m, heads):
                u, n = m // NS, m % NS
                g = NG * b + u
                qh, kt, lo = steps[n]
                if heads[0] == 0:
                    if diagonal[n]:
                        pe.wait_ge(masked, FREE + ND * g + sum(diagonal[:n + 1]))
                    else:
                        pe.wait_ge(exped, 2 * FREE + NE * g + exp_before[n + 1])
                    if n == 0:
                        pe.wait_ge(v_ready, g + 1)
                    if n == first_of[qh]:
                        pe.wait_ge(evacuated, FREE + QH * g + qh)
                for h in heads:
                    last = pe.matmul(pv_ps[32 * h:32 * h + 32, lo:CH], vs[u % 2][:, kt, h, :],
                                     pT[m % PRING][:, h, lo:CH], start=n == first_of[qh], stop=True,
                                     skip_group_check=True)
                if heads[-1] == GH - 1:
                    last.then_inc(weighed, 1)

            def through_bank(b, what, turns):
                if not isinstance(turns, int) or turns:
                    pe.wait_ge(turn_read, turns)
                if what[0] == "max":
                    pe.wait_ge(max_joined, NG * b + what[1] + 1)
                    pe.transpose(t_ps[0:GH * QT, 0:P], negm[:, :], ident).then_inc(max_turned, 1)
                    return
                pe.wait_ge(evacuated, FREE + QH * (NG * b + what[1]) + what[2] + 1)
                for t in range(CT):
                    last = pe.transpose(t_ps[:, t * P:(t + 1) * P], outT[:, t * P:(t + 1) * P], ident)
                last.then_inc(turned, 1)

            def batch(b, last):
                units_at, turns_at = batch_schedule(last)
                turns = 1 + TURNS * b
                for m in range(NG * NS + 2):
                    pieces = []
                    if m < NG * NS:
                        u, n = m // NS, m % NS
                        if n == 0:
                            pe.wait_ge(max_rows[u], 16 * (b + 1))
                        pieces += [(key_scores, b, m, e) for e in range(len(heads_of[n]))]
                    if 0 < m <= NG * NS:
                        pieces += [(weigh, b, m - 1, hs) for hs in ((0, 1), (2, 3))]
                    todo = units_at[m] if m < NG * NS else []
                    for i, (piece, *args) in enumerate(pieces):
                        piece(*args)
                        for r, k in todo[len(todo) * i // len(pieces):len(todo) * (i + 1) // len(pieces)]:
                            if k == 0:
                                pe.wait_ge(loaded[r % NG], LOADS * (b + r // NG + 1))
                            score(NG * b + r, r, k)
                    for what in turns_at[m]:
                        through_bank(b, what, turns)
                        turns = turns + 1

            pe.wait_ge(ones_set, NG)
            pe.wait_ge(loaded[0], LOADS)
            for k in range(NU):
                score(0, 0, k)
            pe.wait_ge(loaded[1], LOADS)
            for k in range(LEAD):
                score(1, 1, k)
                if k == 3:
                    through_bank(0, ("max", 0), 0)
            with pe.Fori(0, B - 1) as b:
                batch(b, False)
            batch(B - 1, True)


class Norm:

    def __init__(self, ctx, nc, taken, name, roots):
        def sb(n, shape):
            return ctx.enter_context(nc.sbuf_tensor(f"{name}_{n}", shape, F32))

        sem = stage_semaphores(nc, ctx, name, taken)

        self.eps, self.neg_half = roots
        self.bst, self.mv = sb("bst", [P, NCH, CT, 6]), sb("mv", [P, NCH, CT, 2])
        self.ve, self.rs = sb("ve", [P, NCH, CT]), sb("rs", [P, NCH, CT])
        self.stats_in, self.mean_var, self.eps_added, self.rooted, self.done = (
            sem(n) for n in ("stats_in", "mean_var", "eps_added", "rooted", "done"))

    def on_vector(self, dve, n0, before, src, dst):
        def stats(c):
            for t in range(CT):
                last = dve.bn_stats(self.bst[:, c, t, :], src(c)[:, t, :])
            last.then_inc(self.stats_in, 1)

        def mean(c):
            for t in range(CT):
                last = dve.bn_aggr(self.mv[:, c, t, :], self.bst[:, c, t, :])
            last.then_inc(self.mean_var, 1)

        def scale(c):
            dve.wait_ge(self.rooted, n0 + c + 1)
            for t in range(CT):
                last = dve.tensor_scalar(dst(c)[:, t, :], src(c)[:, t, :], self.mv[:, c, t, 0:1],
                                         self.rs[:, c, t:t + 1], ALU.subtract, ALU.mult)
            last.then_inc(self.done, 1)

        for c in range(NCH):
            if c >= 2:
                dve.wait_ge(self.stats_in, n0 + c - 1)
            before(c)
            stats(c)
            if c >= 2:
                mean(c - 2)
        for c in range(NCH):
            if c < 2:
                dve.wait_ge(self.stats_in, n0 + NCH - 1 + c)
            scale(c)
            if c < 2:
                mean(NCH - 2 + c)

    def root(self, pool, n, c):
        pool.wait_ge(self.mean_var, n + 1)
        pool.tensor_tensor(self.ve[:, c, :], self.mv[:, c, :, 1], self.eps[:, 0:CT], ALU.add)\
            .then_inc(self.eps_added, 1)
        pool.wait_ge(self.eps_added, n + 1)
        pool.tensor_tensor(self.rs[:, c, :], self.ve[:, c, :], self.neg_half[:, 0:CT], ALU.pow)\
            .then_inc(self.rooted, 1)


def turn(pe, bank, src, ident):
    for t in range(CT):
        last = pe.transpose(bank[:, t * P:(t + 1) * P], src[:, t * P:(t + 1) * P], ident)
    return last


def tokens_out(pe, bank, src, weight):
    for t in range(CT):
        last = pe.matmul(bank[:, t * P:(t + 1) * P], src[:, t * P:(t + 1) * P], weight, start=True, stop=True)
    return last


class Qkv:

    def __init__(self, ctx, nc, taken, name, wq, wk, wv, bq, bk, bv, scr_q, scr_k, v_tm, x32):
        def sb(n, shape, dt):
            return ctx.enter_context(nc.sbuf_tensor(f"{name}_{n}", shape, dt))

        sem = stage_semaphores(nc, ctx, name, taken)

        self.w, self.wv = (wq, wk), wv
        self.b, self.bv, self.scr, self.v_tm, self.x32 = (bq, bk), bv, (scr_q, scr_k), v_tm, x32
        self.part = [sb(f"part{i}", [P, NCH, 3, CH], BF16) for i in range(2)]
        self.mm = [sem("q_mm"), sem("k_mm")]
        self.ev = [sem("q_ev"), sem("k_ev")]
        self.first = [sem("q_first"), sem("k_first")]
        self.rest1 = [sem("q_rest1"), sem("k_rest1")]
        self.second = [sem("q_second"), sem("k_second")]
        self.parted = [sem("q_parted"), sem("k_parted")]
        self.v_mm, self.v_ev = sem("v_mm"), sem("v_ev")
        self.written = [sem(f"written{c}") for c in range(NCH)]

    def pe(self, pe, it, ready, src, bank):
        for s in range(2):
            for c in range(NCH):
                n = NCH * it + c
                if s == 0:
                    pe.wait_ge(ready, n + 1)
                if s == 0:
                    pe.wait_ge(self.v_ev, NCH * it)
                pe.matmul(bank[4 + c if s == 0 else c], self.w[s], src[:, c, :], start=True, stop=True)\
                    .then_inc(self.mm[s], 1)
        for c in range(NCH):
            pe.wait_ge(self.ev[0], NCH * it + c + 1)
            tokens_out(pe, bank[4 + c], src[:, c, :], self.wv).then_inc(self.v_mm, 1)

    def act(self, act, it, bank):
        for s in range(2):
            for c in range(NCH):
                n = NCH * it + c
                act.wait_ge(self.mm[s], n + 1)
                act.wait_ge(self.parted[s], NCH * it)
                act.activation(self.x32[s][:, c, :], bank[4 + c if s == 0 else c], ACT.Identity, bias=self.b[s])\
                    .then_inc(self.ev[s], 1)
        for s in range(2):
            for c in range(NCH):
                act.wait_ge(self.ev[s], NCH * it + c + 1)
                act.wait_ge(self.written[c], 2 * NPROD * 16 * it)
                act.activation(self.part[s][:, c, 0, :], self.x32[s][:, c, :], ACT.Copy)\
                    .then_inc(self.first[s], 1)
        for s in range(2):
            for c in range(NCH):
                act.wait_ge(self.rest1[s], NCH * it + c + 1)
                act.activation(self.part[s][:, c, 1, :], self.x32[s][:, c, :], ACT.Copy)\
                    .then_inc(self.second[s], 1)

    def rest(self, eng, s, it):
        for c in range(NCH):
            eng.wait_ge(self.first[s], NCH * it + c + 1)
            eng.tensor_tensor(self.x32[s][:, c, :], self.x32[s][:, c, :], self.part[s][:, c, 0, :], ALU.subtract)\
                .then_inc(self.rest1[s], 1)
        for c in range(NCH):
            eng.wait_ge(self.second[s], NCH * it + c + 1)
            eng.tensor_tensor(self.part[s][:, c, 2, :], self.x32[s][:, c, :], self.part[s][:, c, 1, :],
                              ALU.subtract).then_inc(self.parted[s], 1)

    def values(self, dve, it, bank):
        for c in range(NCH):
            dve.wait_ge(self.v_mm, NCH * it + c + 1)
            dve.tensor_tensor(self.v_tm[:, chunk_tiles(it, c), :], bank[4 + c].rearrange("p (t f) -> p t f", f=P),
                              self.bv.unsqueeze(1).to_broadcast([P, CT, P]), ALU.add).then_inc(self.v_ev, 1)

    def write(self, sp, it):
        for c in range(NCH):
            for s, order in enumerate((QPART, KPART)):
                sp.wait_ge(self.parted[s], NCH * it + c + 1)
                for j, part in enumerate(order):
                    dst = self.scr[s][j * HD:(j + 1) * HD, :, bass.ds((it * NCH + c) * CH, CH)]
                    sp.dma_start(dst.rearrange("d h t -> (d h) t"), self.part[s][:, c, part, :])\
                        .then_inc(self.written[c], 16)

    def end(self, sp):
        for c in range(NCH):
            sp.wait_ge(self.written[c], 2 * NPROD * 16 * NLOOP)


def rows(t):
    return t.rearrange("p (t f) -> p t f", f=P)


def banks(ps):
    return [ps[:, n * BANK:(n + 1) * BANK] for n in range(8)]


def first_stage(nc, taken, W, C, R, scr_q, scr_k, x_tm, v_tm, ident, roots):
    with ExitStack() as ctx:
        def sb(n, shape=(P, NCH, CH), dt=F32):
            return ctx.enter_context(nc.sbuf_tensor(f"a_{n}", list(shape), dt))

        sem = stage_semaphores(nc, ctx, "a", taken)

        n_tm, xT, q32, k32 = sb("n_tm"), sb("xT"), sb("q32"), sb("k32")
        bank = banks(ctx.enter_context(nc.psum_tensor("a_ps", [P, 8 * BANK], F32)))
        ln = Norm(ctx, nc, taken, "a_ln", roots)
        qkv = Qkv(ctx, nc, taken, "a_qkv", W("q0"), W("k0"), W("v0"), C("bq0"), C("bk0"), R("bv0"),
                  scr_q, scr_k, v_tm, (q32, k32))
        n_turned, x_ready = sem("n_turned"), sem("x_ready")
        block = ctx.enter_context(nc.Block())

        @block.sync
        def _(sp):
            with sp.Fori(0, NLOOP) as it:
                qkv.write(sp, it)
            qkv.end(sp)

        @block.gpsimd
        def _(pool):
            with pool.Fori(0, NLOOP) as it:
                for c in range(NCH):
                    ln.root(pool, NCH * it + c, c)
                qkv.rest(pool, 1, it)

        @block.scalar
        def _(act):
            with act.Fori(0, NLOOP) as it:
                for c in range(NCH):
                    act.wait_ge(n_turned, NCH * it + c + 1)
                    act.activation(xT[:, c, :], bank[c], ACT.Identity, bias=C("b_attn"), scale=C("g_attn"))\
                        .then_inc(x_ready, 1)
                qkv.act(act, it, bank)

        @block.vector
        def _(dve):
            with dve.Fori(0, NLOOP) as it:
                ln.on_vector(dve, NCH * it, lambda c: None, lambda c: x_tm[:, chunk_tiles(it, c), :],
                             lambda c: rows(n_tm[:, c, :]))
                qkv.values(dve, it, bank)
                qkv.rest(dve, 0, it)

        @block.tensor
        def _(pe):
            with pe.Fori(0, NLOOP) as it:
                for c in range(NCH):
                    pe.wait_ge(ln.done, NCH * it + c + 1)
                    pe.wait_ge(qkv.ev[1], NCH * it)
                    turn(pe, bank[c], n_tm[:, c, :], ident).then_inc(n_turned, 1)
                qkv.pe(pe, it, x_ready, xT, bank)


def middle_stage(nc, taken, W, C, R, scr_q, scr_k, x_tm, v_tm, attn_tm, ident, roots, wx_step, w_lin):
    with ExitStack() as ctx:
        def sb(n, shape=(P, NCH, CH), dt=F32):
            return ctx.enter_context(nc.sbuf_tensor(f"m_{n}", list(shape), dt))

        sem = stage_semaphores(nc, ctx, "m", taken)

        at = u = sb("at_u")
        aT = t = sb("aT_t")
        cT = hT = sb("cT_hT")
        x1 = x3 = sb("x1_x3")
        n_tm = sb("n_tm")
        xs = y1 = sb("xs_y1")
        w = y2 = sb("w_y2")
        x2 = y2p = sb("x2_y2p")
        xx = sb("xx")
        hh = [sb(f"hh{i}", (P, 4, CH)) for i in range(2)]
        bank = banks(ctx.enter_context(nc.psum_tensor("m_ps", [P, 8 * BANK], F32)))
        ln1, ln2, ln3, ln4 = (Norm(ctx, nc, taken, f"m_ln{i}", roots) for i in range(1, 5))
        qkv = Qkv(ctx, nc, taken, "m_qkv", W("q1"), W("k1"), W("v1"), C("bq1"), C("bk1"), R("bv1"),
                  scr_q, scr_k, v_tm, (hh[0], hh[1]))
        (at_ready, at_turned, aT_ready, c_mm, cT_ready, c_turned, x1_ready, n1_turned, xs_ready, z_ready,
         tanhed, lagged, sped, moved, xs_turned, xb_ready, x2_ready, xx_ready, n2_turned, hT_ready, f_mm, gelued,
         o_mm, x3_ready, y1_turned, y1T_ready, lin_mm, y2p_ready, y2_turned, y2T_ready, y2_kept) = (sem(n) for n in (
             "at_ready at_turned aT_ready c_mm cT_ready c_turned x1_ready n1_turned xs_ready z_ready tanhed lagged "
             "sped moved xs_turned xb_ready x2_ready xx_ready n2_turned hT_ready f_mm gelued o_mm x3_ready y1_turned "
             "y1T_ready lin_mm y2p_ready y2_turned y2T_ready y2_kept").split())
        block = ctx.enter_context(nc.Block())

        @block.sync
        def _(sp):
            with sp.Fori(0, NLOOP) as it:
                qkv.write(sp, it)
            qkv.end(sp)

        @block.gpsimd
        def _(pool):
            with pool.Fori(0, NLOOP) as it:
                n0 = NCH * it
                for c in range(NCH):
                    ln1.root(pool, n0 + c, c)
                for c in range(NCH):
                    pool.tensor_tensor(rows(xx[:, c, :]), x_tm[:, chunk_tiles(it, c), :],
                                       R("fb2").unsqueeze(1).to_broadcast([P, CT, P]), ALU.add)\
                        .then_inc(xb_ready, 1)
                for k in range(ITERS):
                    for c in range(NCH):
                        m = (ITERS * it + k) * NCH + c
                        pool.wait_ge(tanhed, m + 1)
                        if k:
                            pool.wait_ge(moved, m - NCH + 1)
                        pool.tensor_tensor((t if k else w)[:, c, :], u[:, c, :], xs[:, c, :], ALU.subtract)\
                            .then_inc(lagged, 1)
                for c in range(NCH):
                    pool.wait_ge(x2_ready, n0 + c + 1)
                    pool.wait_ge(xb_ready, n0 + c + 1)
                    pool.tensor_tensor(xx[:, c, :], xx[:, c, :], x2[:, c, :], ALU.add).then_inc(xx_ready, 1)
                for c in range(NCH):
                    ln2.root(pool, n0 + c, c)
                for c in range(NCH):
                    ln3.root(pool, n0 + c, c)
                for c in range(NCH):
                    ln4.root(pool, n0 + c, c)
                qkv.rest(pool, 1, it)

        @block.scalar
        def _(act):
            with act.Fori(0, NLOOP) as it:
                n0 = NCH * it
                for c in range(NCH):
                    act.activation(rows(at[:, c, :]), attn_tm[:, chunk_tiles(it, c), :], ACT.Copy)\
                        .then_inc(at_ready, 1)
                for c in range(NCH):
                    act.wait_ge(at_turned, n0 + c + 1)
                    act.activation(aT[:, c, :], bank[c], ACT.Copy).then_inc(aT_ready, 1)
                for c in range(NCH):
                    act.wait_ge(c_mm, n0 + c + 1)
                    act.activation(cT[:, c, :], bank[4 + c], ACT.Identity, bias=C("bo0")).then_inc(cT_ready, 1)
                for c in range(NCH):
                    act.wait_ge(n1_turned, n0 + c + 1)
                    act.activation(xs[:, c, :], bank[4 + c], ACT.Identity, bias=C("b1"), scale=C("g1"))\
                        .then_inc(xs_ready, 1)
                for k in range(ITERS):
                    for c in range(NCH):
                        m = (ITERS * it + k) * NCH + c
                        act.wait_ge(z_ready, m + 1)
                        act.activation(u[:, c, :], bank[c], ACT.Tanh, bias=C("b_inl")).then_inc(tanhed, 1)
                for c in range(NCH):
                    act.wait_ge(n2_turned, n0 + c + 1)
                    act.activation(hT[:, c, :], bank[c], ACT.Identity, bias=C("b2"), scale=C("g2"))\
                        .then_inc(hT_ready, 1)
                for c in range(NCH):
                    for j in range(4):
                        act.wait_ge(f_mm, 4 * (n0 + c) + j + 1)
                        if c >= 2:
                            act.wait_ge(o_mm, n0 + c - 1)
                        act.activation(hh[c % 2][:, j, :], bank[4 + j], ACT.Gelu, bias=C(f"f{j}"))\
                            .then_inc(gelued, 1)
                for c in range(NCH):
                    act.wait_ge(y1_turned, n0 + c + 1)
                    act.activation(hT[:, c, :], bank[4 + c], ACT.Copy).then_inc(y1T_ready, 1)
                for c in range(NCH):
                    act.wait_ge(y2_turned, n0 + c + 1)
                    act.activation(hT[:, c, :], bank[4 + c], ACT.Copy).then_inc(y2T_ready, 1)
                    act.activation(x_tm[:, chunk_tiles(it, c), :], rows(y2[:, c, :]), ACT.Copy).then_inc(y2_kept, 1)
                qkv.act(act, it, bank)

        @block.vector
        def _(dve):
            def norm(ln, n0, before, src, dst):
                ln.on_vector(dve, n0, before, lambda c: rows(src[:, c, :]), lambda c: rows(dst[:, c, :]))

            with dve.Fori(0, NLOOP) as it:
                n0 = NCH * it
                def before_ln1(c):
                    dve.wait_ge(c_turned, n0 + c + 1)
                    dve.tensor_tensor(rows(x1[:, c, :]), rows(bank[c]), x_tm[:, chunk_tiles(it, c), :], ALU.add)\
                        .then_inc(x1_ready, 1)
                    dve.wait_ge(x1_ready, n0 + c + 1)

                norm(ln1, n0, before_ln1, x1, n_tm)
                for k in range(ITERS):
                    for c in range(NCH):
                        m = (ITERS * it + k) * NCH + c
                        dve.wait_ge(lagged, m + 1)
                        if k:
                            dve.scalar_tensor_tensor(out=w[:, c, :], in0=w[:, c, :], scalar=1.0 - DT, in1=t[:, c, :],
                                                     op0=ALU.mult, op1=ALU.add).then_inc(sped, 1)
                            dve.wait_ge(sped, ((ITERS - 1) * it + k - 1) * NCH + c + 1)
                        dve.scalar_tensor_tensor(out=xs[:, c, :], in0=w[:, c, :], scalar=DT * DT, in1=xs[:, c, :],
                                                 op0=ALU.mult, op1=ALU.add).then_inc(moved, 1)
                def before_ln2(c):
                    dve.wait_ge(xs_turned, n0 + c + 1)
                    dve.tensor_tensor(x2[:, c, :], bank[4 + c], x1[:, c, :], ALU.add).then_inc(x2_ready, 1)
                    dve.wait_ge(x2_ready, n0 + c + 1)

                norm(ln2, n0, before_ln2, x2, n_tm)
                def before_ln3(c):
                    dve.wait_ge(o_mm, n0 + c + 1)
                    dve.wait_ge(xx_ready, n0 + c + 1)
                    dve.tensor_tensor(x3[:, c, :], bank[c], xx[:, c, :], ALU.add).then_inc(x3_ready, 1)
                    dve.wait_ge(x3_ready, n0 + c + 1)

                norm(ln3, n0, before_ln3, x3, y1)
                def before_ln4(c):
                    dve.wait_ge(lin_mm, n0 + c + 1)
                    dve.tensor_tensor(y2p[:, c, :], bank[c], y1[:, c, :], ALU.add).then_inc(y2p_ready, 1)
                    dve.wait_ge(y2p_ready, n0 + c + 1)

                norm(ln4, n0, before_ln4, y2p, y2)
                qkv.values(dve, it, bank)
                qkv.rest(dve, 0, it)

        @block.tensor
        def _(pe):
            with pe.Fori(0, NLOOP) as it:
                n0 = NCH * it
                for c in range(NCH):
                    pe.wait_ge(at_ready, n0 + c + 1)
                    pe.wait_ge(qkv.ev[1], n0)
                    turn(pe, bank[c], at[:, c, :], ident).then_inc(at_turned, 1)
                for c in range(NCH):
                    pe.wait_ge(aT_ready, n0 + c + 1)
                    pe.wait_ge(qkv.v_ev, n0)
                    pe.matmul(bank[4 + c], W("o0"), aT[:, c, :], start=True, stop=True).then_inc(c_mm, 1)
                for c in range(NCH):
                    pe.wait_ge(cT_ready, n0 + c + 1)
                    turn(pe, bank[c], cT[:, c, :], ident).then_inc(c_turned, 1)
                for c in range(NCH):
                    pe.wait_ge(ln1.done, n0 + c + 1)
                    turn(pe, bank[4 + c], n_tm[:, c, :], ident).then_inc(n1_turned, 1)
                for c in range(NCH):
                    pe.wait_ge(xs_ready, n0 + c + 1)
                    pe.matmul(bank[c], W("ctx"), cT[:, c, :], start=True, stop=False)
                    pe.matmul(bank[c], W("x"), xs[:, c, :], start=False, stop=True).then_inc(z_ready, 1)
                for k in range(ITERS - 1):
                    for c in range(NCH):
                        if k:
                            pe.wait_ge(sped, ((ITERS - 1) * it + k - 1) * NCH + c + 1)
                        else:
                            pe.wait_ge(lagged, ITERS * n0 + c + 1)
                        pe.matmul(bank[c], wx_step, w[:, c, :], start=False, stop=True, skip_group_check=True)\
                            .then_inc(z_ready, 1)
                for c in range(NCH):
                    pe.wait_ge(moved, (ITERS * it + ITERS - 1) * NCH + c + 1)
                    turn(pe, bank[4 + c], xs[:, c, :], ident).then_inc(xs_turned, 1)
                for c in range(NCH):
                    pe.wait_ge(ln2.done, n0 + c + 1)
                    turn(pe, bank[c], n_tm[:, c, :], ident).then_inc(n2_turned, 1)

                def down(c):
                    pe.wait_ge(gelued, 4 * (n0 + c) + 4)
                    for i in range(CT):
                        for j in range(4):
                            last = pe.matmul(bank[c][:, i * P:(i + 1) * P], hh[c % 2][:, j, i * P:(i + 1) * P],
                                             W("f2")[:, j * P:(j + 1) * P], start=j == 0, stop=j == 3)
                    last.then_inc(o_mm, 1)

                pe.wait_ge(x2_ready, n0 + NCH)
                for c in range(NCH):
                    pe.wait_ge(hT_ready, n0 + c + 1)
                    for j in range(4):
                        if c:
                            pe.wait_ge(gelued, 4 * (n0 + c - 1) + j + 1)
                        pe.matmul(bank[4 + j], W("f1")[:, j * P:(j + 1) * P], hT[:, c, :], start=True, stop=True)\
                            .then_inc(f_mm, 1)
                    if c:
                        down(c - 1)
                down(NCH - 1)
                for c in range(NCH):
                    pe.wait_ge(ln3.done, n0 + c + 1)
                    turn(pe, bank[4 + c], y1[:, c, :], ident).then_inc(y1_turned, 1)
                for c in range(NCH):
                    pe.wait_ge(y1T_ready, n0 + c + 1)
                    tokens_out(pe, bank[c], hT[:, c, :], w_lin).then_inc(lin_mm, 1)
                for c in range(NCH):
                    pe.wait_ge(ln4.done, n0 + c + 1)
                    turn(pe, bank[4 + c], y2[:, c, :], ident).then_inc(y2_turned, 1)
                qkv.pe(pe, it, y2T_ready, hT, bank)


def last_stage(nc, taken, W, C, R, out, x_tm, attn_tm, ident, roots):
    with ExitStack() as ctx:
        def sb(n, shape=(P, NCH, CH), dt=F32):
            return ctx.enter_context(nc.sbuf_tensor(f"e_{n}", list(shape), dt))

        sem = stage_semaphores(nc, ctx, "e", taken)

        at, aT, xb, x1, y3, yb, hT, x4, y4 = (sb(n) for n in "at aT xb x1 y3 yb hT x4 y4".split())
        hh = [sb(f"hh{i}", (P, 4, CH)) for i in range(2)]
        bank = banks(ctx.enter_context(nc.psum_tensor("e_ps", [P, 8 * BANK], F32)))
        ln5, ln6 = (Norm(ctx, nc, taken, f"e_ln{i}", roots) for i in (5, 6))
        (at_ready, at_turned, aT_ready, o_mm, xb_ready, x1_ready, yb_ready, y3_turned, hT_ready, f_mm, relued, d_mm,
         x4_ready) = (sem(n) for n in ("at_ready at_turned aT_ready o_mm xb_ready x1_ready yb_ready y3_turned "
                                       "hT_ready f_mm relued d_mm x4_ready").split())
        stored = [sem(f"stored{c}") for c in range(NCH)]
        block = ctx.enter_context(nc.Block())

        @block.sync
        def _(sp):
            with sp.Fori(0, NLOOP) as it:
                for c in range(NCH):
                    sp.wait_ge(ln6.done, NCH * it + c + 1)
                    sp.dma_start(out.rearrange("b (n p) d -> p (b n) d", p=P)[:, chunk_tiles(it, c), :],
                                 rows(y4[:, c, :])).then_inc(stored[c], 16)
            for c in range(NCH):
                sp.wait_ge(stored[c], 16 * NLOOP)

        @block.gpsimd
        def _(pool):
            with pool.Fori(0, NLOOP) as it:
                n0 = NCH * it
                for c in range(NCH):
                    pool.tensor_tensor(rows(xb[:, c, :]), x_tm[:, chunk_tiles(it, c), :],
                                       R("bo1").unsqueeze(1).to_broadcast([P, CT, P]), ALU.add)\
                        .then_inc(xb_ready, 1)
                for c in range(NCH):
                    ln5.root(pool, n0 + c, c)
                for c in range(NCH):
                    pool.wait_ge(ln5.done, n0 + c + 1)
                    pool.tensor_tensor(rows(yb[:, c, :]), rows(y3[:, c, :]),
                                       R("hb2").unsqueeze(1).to_broadcast([P, CT, P]), ALU.add)\
                        .then_inc(yb_ready, 1)
                for c in range(NCH):
                    ln6.root(pool, n0 + c, c)

        @block.scalar
        def _(act):
            with act.Fori(0, NLOOP) as it:
                n0 = NCH * it
                for c in range(NCH):
                    act.activation(rows(at[:, c, :]), attn_tm[:, chunk_tiles(it, c), :], ACT.Copy)\
                        .then_inc(at_ready, 1)
                for c in range(NCH):
                    act.wait_ge(at_turned, n0 + c + 1)
                    act.activation(aT[:, c, :], bank[c], ACT.Copy).then_inc(aT_ready, 1)
                for c in range(NCH):
                    act.wait_ge(y3_turned, n0 + c + 1)
                    act.activation(hT[:, c, :], bank[c], ACT.Copy).then_inc(hT_ready, 1)
                for c in range(NCH):
                    for j in range(4):
                        act.wait_ge(f_mm, 4 * (n0 + c) + j + 1)
                        if c >= 2:
                            act.wait_ge(d_mm, n0 + c - 1)
                        act.activation(hh[c % 2][:, j, :], bank[4 + j], ACT.Relu, bias=C(f"h{j}"))\
                            .then_inc(relued, 1)

        @block.vector
        def _(dve):
            def norm(ln, n0, before, src, dst):
                ln.on_vector(dve, n0, before, lambda c: rows(src[:, c, :]), lambda c: rows(dst[:, c, :]))

            with dve.Fori(0, NLOOP) as it:
                n0 = NCH * it

                def before_ln5(c):
                    dve.wait_ge(o_mm, n0 + c + 1)
                    dve.wait_ge(xb_ready, n0 + c + 1)
                    dve.tensor_tensor(x1[:, c, :], bank[4 + c], xb[:, c, :], ALU.add).then_inc(x1_ready, 1)
                    dve.wait_ge(x1_ready, n0 + c + 1)

                norm(ln5, n0, before_ln5, x1, y3)

                def before_ln6(c):
                    dve.wait_ge(d_mm, n0 + c + 1)
                    dve.wait_ge(yb_ready, n0 + c + 1)
                    dve.tensor_tensor(x4[:, c, :], bank[c], yb[:, c, :], ALU.add).then_inc(x4_ready, 1)
                    dve.wait_ge(x4_ready, n0 + c + 1)

                for c in range(NCH):
                    dve.wait_ge(stored[c], 16 * it)
                norm(ln6, n0, before_ln6, x4, y4)

        @block.tensor
        def _(pe):
            with pe.Fori(0, NLOOP) as it:
                n0 = NCH * it
                for c in range(NCH):
                    pe.wait_ge(at_ready, n0 + c + 1)
                    pe.wait_ge(x4_ready, n0)
                    turn(pe, bank[c], at[:, c, :], ident).then_inc(at_turned, 1)
                for c in range(NCH):
                    pe.wait_ge(aT_ready, n0 + c + 1)
                    pe.wait_ge(relued, 4 * n0)
                    tokens_out(pe, bank[4 + c], aT[:, c, :], W("o1")).then_inc(o_mm, 1)
                for c in range(NCH):
                    pe.wait_ge(ln5.done, n0 + c + 1)
                    turn(pe, bank[c], y3[:, c, :], ident).then_inc(y3_turned, 1)

                def down(c):
                    pe.wait_ge(relued, 4 * (n0 + c) + 4)
                    for i in range(CT):
                        for j in range(4):
                            last = pe.matmul(bank[c][:, i * P:(i + 1) * P], hh[c % 2][:, j, i * P:(i + 1) * P],
                                             W("g2")[:, j * P:(j + 1) * P], start=j == 0, stop=j == 3)
                    last.then_inc(d_mm, 1)

                pe.wait_ge(x1_ready, n0 + NCH)
                for c in range(NCH):
                    pe.wait_ge(hT_ready, n0 + c + 1)
                    for j in range(4):
                        if c:
                            pe.wait_ge(relued, 4 * (n0 + c - 1) + j + 1)
                        pe.matmul(bank[4 + j], W("g1")[:, j * P:(j + 1) * P], hT[:, c, :], start=True, stop=True)\
                            .then_inc(f_mm, 1)
                    if c:
                        down(c - 1)
                down(NCH - 1)


def two_layer_kernel(nc, x, w_pack, c_pack, r_pack, out):
    scr = [nc.dram_tensor(f"scr_{n}", [ROWS, H, TOK], BF16, kind="Internal").ap() for n in ("q0", "k0", "q1", "k1")]
    scr_m = [nc.dram_tensor(f"scr_m{i}", [3, B * H * QT, P], BF16, kind="Internal").ap() for i in range(2)]
    with ExitStack() as ctx:
        def sb(n, shape, dt=F32):
            return ctx.enter_context(nc.sbuf_tensor(n, shape, dt))

        def sem(n):
            return ctx.enter_context(nc.semaphore(n))

        x_tm = sb("x_tm", [P, TILES, D])
        v_tm = sb("v_tm", [P, TILES, D])
        attn_tm = sb("attn_tm", [P, TILES, D])
        w_sb = sb("w_sb", [P, W_COLS])
        c_sb = sb("c_sb", [P, len(C_AT)])
        r_sb = sb("r_sb", [P, len(R_AT), D])
        wx_step = sb("wx_step", [P, D])
        w_lin = sb("w_lin", [P, D])
        ident = sb("ident", [P, P])
        ident_bf = sb("ident_bf", [P, P], BF16)
        mask_neg = sb("mask_neg", [P, P], BF16)
        roots = [sb("eps", [P, CT]), sb("neg_half", [P, CT])]

        def W(n):
            at, width = W_AT[n]
            return w_sb[:, at:at + width]

        def C(n):
            return c_sb[:, C_AT[n]:C_AT[n] + 1]

        def R(n):
            return r_sb[:, R_AT[n], :]

        x_in, w_in, small_in, blank, cut_out = (sem(n) for n in "x_in w_in small_in blank cut_out".split())
        with nc.Block() as block:
            @block.sync
            def _(sp):
                sp.dma_start(c_sb[:, :], c_pack).then_inc(small_in, 16)
                sp.dma_start(r_sb[:, :, :], r_pack.unsqueeze(0).to_broadcast([P, len(R_AT), D])).then_inc(small_in, 16)
                for b in range(B):
                    sp.dma_start(x_tm[:, b * QT:(b + 1) * QT, :],
                                 x[b, :, :].rearrange("(n p) d -> p n d", p=P)).then_inc(x_in, 16)
                sp.wait_ge(small_in, 32)
                sp.wait_ge(x_in, 16 * B)

            @block.scalar
            def _(act):
                act.dma_start(w_sb[:, :], w_pack).then_inc(w_in, 16)

            @block.gpsimd
            def _(pool):
                pool.memset(ident[:, :], 0.0).then_inc(blank, 1)
                pool.memset(mask_neg[:, :], 0.0).then_inc(blank, 1)
                pool.memset(roots[0][:, :], EPS)
                pool.memset(roots[1][:, :], -0.5)
                pool.wait_ge(blank, 2)
                pool.affine_select(out=ident[:, :], in_=ident[:, :], compare_op=ALU.not_equal, fill=1.0, base=0,
                                   pattern=[[-1, P]], channel_multiplier=1).then_inc(cut_out, 1)
                pool.affine_select(out=mask_neg[:, :], in_=mask_neg[:, :], compare_op=ALU.is_ge, fill=-3.0e38, base=0,
                                   pattern=[[-1, P]], channel_multiplier=1).then_inc(cut_out, 1)

            @block.vector
            def _(dve):
                dve.wait_ge(cut_out, 1)
                dve.tensor_copy(ident_bf[:, :], ident[:, :])
                dve.wait_ge(w_in, 16)
                dve.tensor_scalar(wx_step[:, :], W("x"), DT * DT, None, ALU.mult)
                dve.tensor_tensor(w_lin[:, :], W("lin"), W("dis"), ALU.add)

        taken = []
        first_stage(nc, taken, W, C, R, scr[0], scr[1], x_tm, v_tm, ident[:, :], roots)
        attention(nc, taken, "l0", True, scr[0], scr[1], scr_m[0], v_tm, attn_tm, ident[:, :], mask_neg[:, :],
                  ident_bf[:, :])
        retire(nc, taken)
        middle_stage(nc, [], W, C, R, scr[2], scr[3], x_tm, v_tm, attn_tm, ident[:, :], roots, wx_step[:, :],
                     w_lin[:, :])
        attention(nc, [], "l1", False, scr[2], scr[3], scr_m[1], v_tm, attn_tm, ident[:, :], mask_neg[:, :],
                  ident_bf[:, :])
        last_stage(nc, [], W, C, R, out, x_tm, attn_tm, ident[:, :], roots)


def kernel(**inputs):
    import numpy as np
    import concourse.bacc as bacc
    from concourse import mybir as mb
    from concourse.bass_utils import run_bass_kernel_spmd

    a = {n: np.asarray(v) for n, v in inputs.items()}

    def by_dim(w):
        return w.reshape(w.shape[:-1] + (H, HD)).swapaxes(-1, -2).reshape(w.shape)

    def parts0(w):
        q, k, v = (w[..., n * D:(n + 1) * D] for n in range(3))
        return by_dim(q), by_dim(k), v

    def parts1(w):
        w = w.reshape(w.shape[:-1] + (H, 3, HD))
        q, k, v = (w[..., n, :].reshape(w.shape[:-3] + (D,)) for n in range(3))
        return by_dim(q), by_dim(k), v

    def by_rows(w):
        return w.reshape(4, P, D).transpose(1, 0, 2).reshape(P, 4 * D)

    disha = a["L0_ffn_disha"]
    w_pack = np.concatenate([
        *parts0(a["L0_attn_qkv_w"]), a["L0_attn_out_w"], a["L0_attn_w_ctx"], a["L0_attn_w_x"], a["L0_attn_ff_w1"],
        by_rows(a["L0_attn_ff_w2"]), a["L0_ffn_weight"].T, np.concatenate([disha, disha], axis=0),
        *parts1(a["L1_attn_Wqkv"]), a["L1_attn_Wout"], a["L1_ffn_W1"], by_rows(a["L1_ffn_W2"])], axis=1)
    bq0, bk0, bv0 = parts0(a["L0_attn_qkv_b"])
    bq1, bk1, bv1 = parts1(a["L1_attn_bqkv"])
    c_pack = np.stack([
        bq0, bk0, a["L0_attn_out_b"], a["L0_attn_g_attn"], a["L0_attn_b_attn"], a["L0_attn_g1"], a["L0_attn_b1"],
        a["L0_attn_g2"], a["L0_attn_b2"], a["L0_attn_b_inl"], *a["L0_attn_ff_b1"].reshape(4, P),
        bq1, bk1, *a["L1_ffn_b1"].reshape(4, P)], axis=1)
    r_pack = np.stack([bv0, a["L0_attn_ff_b2"], bv1, a["L1_attn_bout"], a["L1_ffn_b2"]])

    nc = bacc.Bacc("TRN2", target_bir_lowering=False, num_devices=1)
    arrays, args = {}, []
    for name, v in (("x", a["L0_attn_x"]), ("w_pack", w_pack), ("c_pack", c_pack), ("r_pack", r_pack)):
        v = np.ascontiguousarray(v)
        arrays[f"in_{name}"] = v
        args.append(nc.dram_tensor(f"in_{name}", v.shape, mb.dt.from_np(v.dtype), kind="ExternalInput").ap())
    args.append(nc.dram_tensor("out_0", (B, SEQ, D), mb.dt.float32, kind="ExternalOutput").ap())
    two_layer_kernel(nc, *args)
    r = run_bass_kernel_spmd(nc, [arrays], core_ids=[0])
    return r.results[0]["out_0"]
```

```python
import concourse.bass as bass
from concourse import mybir
from contextlib import ExitStack

F32 = mybir.dt.float32
BF16 = mybir.dt.bfloat16
ALU = mybir.AluOpType
ACT = mybir.ActivationFunctionType
AX_X = mybir.AxisListType.X

P = 128
B, SEQ, D = 4, 1024, 128
H, HD = 16, 8
FF = 512
ITERS = 8
DT = 0.1
EPS = 1e-5
TOK = B * SEQ
TILES = TOK // P
BANK = 512
CH = 512
CT = CH // P
NCH = 4
NLOOP = TOK // (CH * NCH)

QPART = (0, 0, 0, 1, 1, 2)
KPART = (0, 1, 2, 0, 1, 0)
NPROD = len(QPART)
PARTS = 3
MROW = 96
GH = 4
NG = H // GH
QT = SEQ // P
QH = SEQ // CH
SCALE = 1.0 / float(HD) ** 0.5
BF16_ONES = 1.0 + 0x3F80 / 2 ** 23
FREE = 1


def part_runs(order):
    out = []
    for j, part in enumerate(order):
        if out and part == order[j - 1] + 1:
            out[-1][2] += 1
        else:
            out.append([j, part, 1])
    return out


LOADS = 16 * (len(part_runs(QPART)) + len(part_runs(KPART)))

W_AT = {}
_at = 0
for _n, _w in (("q0", D), ("k0", D), ("v0", D), ("o0", D), ("ctx", D), ("x", D), ("f1", FF), ("f2", FF),
               ("lin", D), ("dis", D), ("q1", D), ("k1", D), ("v1", D), ("o1", D), ("g1", FF), ("g2", FF)):
    W_AT[_n] = (_at, _w)
    _at += _w
W_COLS = _at
C_AT = {n: i for i, n in enumerate(
    ("bq0", "bk0", "bo0", "g_attn", "b_attn", "g1", "b1", "g2", "b2", "b_inl", "f0", "f1", "f2", "f3",
     "bq1", "bk1", "h0", "h1", "h2", "h3"))}
R_AT = {n: i for i, n in enumerate(("bv0", "fb2", "bv1", "bo1", "hb2"))}


def chunk_tiles(it, c):
    return bass.ds((it * NCH + c) * CT, CT)


def attention_steps(causal):
    return [(qh, kt, max(0, kt * P - qh * CH) if causal else 0) for qh in range(QH) for kt in range(QT)
            if not causal or kt * P < (qh + 1) * CH]


def score_units(causal):
    out = []
    for h in range(GH):
        for qt in range(QT):
            keys = (qt + 1) * P if causal else SEQ
            for n, at in enumerate(range(0, keys, BANK)):
                w = min(BANK, keys - at)
                if h % (BANK // w) == 0:
                    out.append((tuple(range(h, h + BANK // w)), qt, n, at, w))
    return out


def stage_semaphores(nc, ctx, prefix, taken):
    def sem(n):
        taken.append(ctx.enter_context(nc.semaphore(f"{prefix}_{n}")))
        return taken[-1]
    return sem


def retire(nc, taken):
    with nc.Block() as block:
        @block.sync
        def _(sp):
            for s in taken:
                sp.sem_clear(s)


def load_group(sp, scr, slots, loaded, b, u):
    for side, order in enumerate((QPART, KPART)):
        for j, part, n in part_runs(order):
            sp.dma_start(slots[side][u][j * HD:(j + n) * HD, :, :],
                         scr[side][part * HD:(part + n) * HD, u * GH:(u + 1) * GH, bass.ds(b * SEQ, SEQ)])\
                .then_inc(loaded[u], 16)


def attention(nc, taken, name, causal, scr, scr_m, slots, loaded, written, v_tm, attn_tm, ident, mask_neg, ident_bf):
    steps = attention_steps(causal)
    units = score_units(causal)
    NS, NU = len(steps), len(units)
    first_of = [min(n for n, s in enumerate(steps) if s[0] == qh) for qh in range(QH)]
    last_of = [max(n for n, s in enumerate(steps) if s[0] == qh) for qh in range(QH)]
    heads_of = [[tuple(range(h, h + BANK // (CH - lo))) for h in range(0, GH, BANK // (CH - lo))]
                for _, _, lo in steps]
    exp_before = [sum(len(x) for x in heads_of[:n]) for n in range(NS + 1)]
    NE = exp_before[NS]
    diagonal = [causal and kt * P >= qh * CH for qh, kt, _ in steps]
    ND = sum(diagonal)
    PRING = 4
    SRING, ERING = 3, 3
    WEIGH = GH
    assert (NG * NS) % PRING == 0

    def since_last(k, units_of_group, ring):
        return ring if k >= ring else k + 1 + (units_of_group - 1 - k) % ring
    LEAD = NU * (9 if causal else 6) // 20

    WLAG = 2
    pieces = []
    for m in range(NG * NS + WLAG):
        pieces.append([])
        if m < NG * NS:
            pieces[m] += [("key", m, e) for e in range(len(heads_of[m % NS]))]
        if m >= WLAG:
            half = (len(pieces[m]) + 1) // 2
            pieces[m][half:half] = [("weigh", m - WLAG, h) for h in range(0, GH, WEIGH)]

    def piece_cost(kind, m, n):
        return (CH - steps[m % NS][2]) * (WEIGH if kind == "weigh" else len(heads_of[m % NS][n]))

    stream = [(1 + (LEAD + i) // NU, (LEAD + i) % NU) for i in range(NG * NU)]
    weight = [len(units[k][0]) * units[k][4] + 64 for _, k in stream]
    cost_sum = sum(piece_cost(*x) for ps in pieces[:NG * NS] for x in ps)
    units_after, at, so_far = [[[] for _ in ps] for ps in pieces], 0, 0
    for m in range(NG * NS):
        for i, x in enumerate(pieces[m]):
            so_far += piece_cost(*x)
            while at < len(stream) and (sum(weight[:at]) + weight[at] / 2) / sum(weight) < so_far / cost_sum:
                units_after[m][i].append(stream[at])
                at += 1
    assert at == len(stream)
    through = [[] for _ in range(NG * NS + WLAG + 1)]
    for u in range(NG):
        for qh in range(QH):
            through[u * NS + last_of[qh] + WLAG + 1].append(("out", u, qh))
    for m in range(NG * NS):
        for r, k in sum(units_after[m], []):
            if k == NU - 1:
                at = m + 1
                while through[at]:
                    at += 1
                through[at].append(("max", r))

    def batch_schedule(last):
        keep = (lambda r: r < NG) if last else (lambda r: True)
        return ([[[x for x in after if keep(x[0])] for after in step] for step in units_after],
                [[x for x in t if x[0] == "out" or keep(x[1])] for t in through])

    def count(per_group, b, u, more):
        return NG * per_group * b + (per_group * u + more)

    def count_units(b, r, more):
        return NG * NU * (b + 1) + (NU * (r - NG) + more)

    TURNS = sum(len(t) for t in through)

    with ExitStack() as ctx:
        def sb(n, shape, dt):
            return ctx.enter_context(nc.sbuf_tensor(f"{name}_{n}", shape, dt))

        sem = stage_semaphores(nc, ctx, name, taken)
        Qs, Ks = slots
        pT = [sb(f"pT{i}", [P, GH, CH], F32) for i in range(PRING)]
        vs = [sb(f"vs{i}", [P, QT, GH, 32], F32) for i in range(2)]
        negp = [sb(f"negp{i}", [P, GH * QT, 2], F32) for i in range(2)]
        negm = sb("negm", [P, GH * QT], F32)
        msp = sb("msp", [GH * QT, 3, P], BF16)
        mres = sb("mres", [GH * QT, 2, P], F32)
        outT = sb("outT", [P, CH], F32)
        rc = sb("rc", [P, CT, GH], F32)
        held = sb("held", [P, 2], F32)
        ps = ctx.enter_context(nc.psum_tensor(f"{name}_ps", [P, 8 * BANK], F32))
        FIRST_RING = SRING + ERING
        st_ps = [ps[:, n * BANK:(n + 1) * BANK] for n in range(SRING, SRING + ERING)]
        pv_ps = ps[:, 6 * BANK:7 * BANK]
        t_ps = ps[:, 7 * BANK:8 * BANK]

        max_rows = [sem(f"max_rows{i}") for i in range(NG)]
        scored = sem("scored")
        reduced = sem("reduced")
        keyed = sem("keyed")
        exped = sem("exped")
        masked = sem("masked")
        weighed = sem("weighed")
        evacuated = sem("evacuated")
        turned = sem("turned")
        recips = sem("recips")
        turn_read = sem("turn_read")
        max_joined = sem("max_joined")
        max_turned = sem("max_turned")
        max_part = sem("max_part")
        max_split = sem("max_split")
        max_stored = sem("max_stored")
        v_clear = sem("v_clear")
        v_ready = sem("v_ready")
        block = ctx.enter_context(nc.Block())

        @block.sync
        def _(sp):
            def put_max(b, u):
                sp.wait_ge(max_split, count(1, b, u, 1))
                mine = scr_m[:, bass.ds(count(GH * QT, b, u, 0), GH * QT), :]
                sp.dma_start(mine.rearrange("s r c -> r s c"), msp[:, :, :]).then_inc(max_stored, 16)
                sp.wait_ge(max_stored, count(16, b, u, 16))
                sp.dma_start(Qs[u % NG][MROW:MROW + 3, :, :].rearrange("p h (t c) -> p (h t) c", c=P), mine)\
                    .then_inc(max_rows[u % NG], 16)

            def body(b, u, ahead):
                if ahead >= 3:
                    sp.wait_ge(keyed, count(NE, b, u, 1))
                    load_group(sp, scr, slots, loaded, b + (u + 3) // NG, (u + 3) % NG)
                if ahead >= 1:
                    put_max(b, u + 1)

            for c in range(NCH):
                sp.wait_ge(written[c], 2 * 16 * NLOOP + FREE)
            put_max(0, 0)
            with sp.Fori(0, B - 1) as b:
                for u in range(NG):
                    body(b, u, NG)
            for u in range(NG):
                body(B - 1, u, NG - 1 - u)

        @block.gpsimd
        def _(pool):
            def values(b, u):
                pool.tensor_copy(vs[u % 2][:, :, :, 0:HD],
                                 v_tm[:, bass.ds(b * QT, QT), u * GH * HD:(u + 1) * GH * HD]
                                 .rearrange("p t (h d) -> p t h d", d=HD)).then_inc(v_ready, 1)

            def body(b, u, more):
                for n, (qh, kt, lo) in enumerate(steps):
                    if n == 4 and more:
                        pool.wait_ge(weighed, count(NS, b, u, PRING + 1))
                        values(b + (u + 1) // NG, (u + 1) % NG)
                    if diagonal[n]:
                        pool.wait_ge(masked, count(ND, b, u, FREE + sum(diagonal[:n])))
                        pool.wait_ge(exped, count(NE, b, u, ERING + exp_before[n + 1]))
                        pool.tensor_tensor(held[:, 0:1], held[:, 1:2], held[:, 1:2], ALU.mult)
                        blk = pT[(u * NS + n) % PRING][:, :, lo:lo + P]
                        pool.affine_select(out=blk, in_=blk, compare_op=ALU.is_ge, fill=0.0, base=0,
                                           pattern=[[0, GH], [1, P]], channel_multiplier=-1)\
                            .then_inc(masked, 1)

            pool.memset(held[:, :], 0.0).then_inc(masked, FREE)
            for i in range(2):
                pool.memset(vs[i][:, :, :, :], 0.0).then_inc(v_clear, 1)
            pool.wait_ge(v_clear, 2)
            for i in range(2):
                pool.memset(vs[i][:, :, :, HD:HD + 1], 1.0).then_inc(v_clear, 1)
            pool.wait_ge(v_clear, 4)
            values(0, 0)
            with pool.Fori(0, B - 1) as b:
                for u in range(NG):
                    body(b, u, True)
            for u in range(NG):
                body(B - 1, u, u < NG - 1)

        @block.scalar
        def _(act):
            def evacuate(b, u, qh):
                act.wait_ge(weighed, count(NS, b, u, PRING + last_of[qh] + 1))
                act.wait_ge(turned, count(QH, b, u, FREE + qh))
                act.activation(outT[:, :], pv_ps, ACT.Copy).then_inc(evacuated, 1)

            with act.Fori(0, B) as b:
                due = {}
                for m in range(NG * NS):
                    u, n = m // NS, m % NS
                    qh, kt, lo = steps[n]
                    act.wait_ge(weighed, count(NS, b, 0, m + 1))
                    for e, hs in enumerate(heads_of[n]):
                        k = exp_before[n] + e
                        if e and e == (len(heads_of[n]) + 1) // 2 and m in due:
                            evacuate(*due.pop(m))
                        act.wait_ge(keyed, count(NE, b, u, k + 1))
                        src = st_ps[k % ERING].rearrange("p (h c) -> p h c", h=len(hs))[:, :, 0:CH - lo]
                        act.activation(pT[m % PRING][:, hs[0]:hs[-1] + 1, lo:CH], src, ACT.Exp, scale=SCALE)\
                            .then_inc(exped, 1)
                    if n == last_of[qh]:
                        due[m + WLAG] = (b, u, qh)
                    if m in due:
                        evacuate(*due.pop(m))
                evacuate(*due[NG * NS - 1 + WLAG])

        @block.vector
        def _(dve):
            def reduce(b, r, k, bank):
                hs, qt, part, at, w = units[k]
                dve.wait_ge(scored, count_units(b, r, k + 1))
                dst = negp[r % 2].rearrange("p (h t) n -> p h t n", h=GH)[:, hs[0]:hs[-1] + 1, qt, part]
                src = ps[:, bank * BANK:bank * BANK + len(hs) * w].rearrange("p (h k) -> p h k", h=len(hs))
                dve.tensor_reduce(dst, src, AX_X, ALU.max, negate=True).then_inc(reduced, 1)
                if k == NU - 1:
                    join(b, r)

            def join(b, r):
                dve.wait_ge(reduced, count_units(b, r, NU))
                if not isinstance(b, int) or b or r:
                    dve.wait_ge(max_turned, count(1, b, r, 0))
                dve.tensor_tensor(negm[:, :], negp[r % 2][:, :, 0], negp[r % 2][:, :, 1], ALU.min)\
                    .then_inc(max_joined, 1)

            def split(b, r, turns):
                src = t_ps[0:GH * QT, 0:P]
                dve.wait_ge(max_turned, count(1, b, r, 1))
                if not isinstance(b, int) or b or r:
                    dve.wait_ge(max_stored, count(16, b, r, 0))
                dve.tensor_copy(msp[:, 0, :], src).then_inc(max_part, 1)
                dve.wait_ge(max_part, count(3, b, r, 1))
                dve.tensor_tensor(mres[:, 0, :], src, msp[:, 0, :], ALU.subtract).then_inc(turn_read, 1)
                dve.wait_ge(turn_read, turns + 1)
                dve.tensor_copy(msp[:, 1, :], mres[:, 0, :]).then_inc(max_part, 1)
                dve.wait_ge(max_part, count(3, b, r, 2))
                dve.tensor_tensor(mres[:, 1, :], mres[:, 0, :], msp[:, 1, :], ALU.subtract).then_inc(max_part, 1)
                dve.wait_ge(max_part, count(3, b, r, 3))
                dve.tensor_copy(msp[:, 2, :], mres[:, 1, :]).then_inc(max_split, 1)

            def norm(b, u, qh):
                src = t_ps.rearrange("p (t h c) -> p t h c", t=CT, h=GH)
                dve.wait_ge(turned, count(QH, b, u, FREE + qh + 1))
                dve.reciprocal(rc[:, :, :], src[:, :, :, HD]).then_inc(recips, 1)
                dve.wait_ge(recips, count(QH, b, u, qh + 1))
                dst = attn_tm[:, bass.ds(b * QT + qh * CT, CT), u * GH * HD:(u + 1) * GH * HD]
                dve.tensor_tensor(dst.rearrange("p t (h d) -> p t h d", d=HD), src[:, :, :, 0:HD],
                                  rc[:, :, :].unsqueeze(3).to_broadcast([P, CT, GH, HD]), ALU.mult)\
                    .then_inc(turn_read, 1)

            def batch(b, last):
                units_at, turns_at = batch_schedule(last)
                turns = 1
                for m in range(NG * NS + WLAG + 1):
                    for what in turns_at[m - 1] if m else ():
                        if what[0] == "max":
                            split(b, what[1], TURNS * b + turns)
                        else:
                            norm(b, what[1], what[2])
                        turns = turns + 1
                    for r, k in sum(units_at[m], []) if m < NG * NS else ():
                        reduce(b, r, k, k % SRING)
                for what in turns_at[-1]:
                    norm(b, what[1], what[2])

            dve.memset(negp[0][:, :, 1], 3.0e38).then_inc(exped, ERING)
            dve.memset(negp[1][:, :, 1], 3.0e38).then_inc(weighed, PRING)
            dve.memset(rc[:, :, :], 0.0).then_inc(evacuated, FREE)
            dve.memset(negm[:, :], 0.0).then_inc(turned, FREE)
            for started, credit in ((exped, ERING), (weighed, PRING), (evacuated, FREE), (turned, FREE)):
                dve.wait_ge(started, credit)
            for k in range(NU):
                reduce(0, 0, k, k % FIRST_RING)
            for k in range(LEAD):
                reduce(0, 1, k, k % SRING)
                if k == 4:
                    split(0, 0, 0)
            with dve.Fori(0, B - 1) as b:
                batch(b, False)
            batch(B - 1, True)

        @block.tensor
        def _(pe):
            def score(b, r, k, bank, since):
                hs, qt, part, at, w = units[k]
                n = count_units(b, r, k - since + 1)
                if not isinstance(n, int) or n > 0:
                    pe.wait_ge(reduced, n)
                s = r % NG
                diag = causal and at + w == (qt + 1) * P
                for i, h in enumerate(hs):
                    out = ps[:, bank * BANK + i * w:bank * BANK + (i + 1) * w]
                    last = pe.matmul(out, Qs[s][0:MROW, h, qt * P:(qt + 1) * P], Ks[s][0:MROW, h, at:at + w],
                                     start=True, stop=True)
                    if diag:
                        last = pe.matmul(out[:, w - P:w], ident_bf, mask_neg, start=False, stop=True,
                                         skip_group_check=True)
                last.then_inc(scored, 1)

            def key_scores(b, m, e):
                u, n = m // NS, m % NS
                qh, kt, lo = steps[n]
                hs, k, w = heads_of[n][e], exp_before[n] + e, CH - lo
                pe.wait_ge(exped, count(NE, b, u, ERING + k + 1 - since_last(k, NE, ERING)))
                out = st_ps[k % ERING].rearrange("p (h c) -> p h c", h=len(hs))
                for i, h in enumerate(hs):
                    last = pe.matmul(out[:, i, 0:w], Ks[u][:, h, kt * P:(kt + 1) * P],
                                     Qs[u][:, h, qh * CH + lo:(qh + 1) * CH], start=True, stop=True)
                last.then_inc(keyed, 1)

            def weigh(b, m, heads):
                u, n = m // NS, m % NS
                qh, kt, lo = steps[n]
                if heads[0] == 0:
                    if diagonal[n]:
                        pe.wait_ge(masked, count(ND, b, u, FREE + sum(diagonal[:n + 1])))
                    else:
                        pe.wait_ge(exped, count(NE, b, u, ERING + exp_before[n + 1]))
                    if n == 0:
                        pe.wait_ge(v_ready, count(1, b, u, 1))
                    if n == first_of[qh]:
                        pe.wait_ge(evacuated, count(QH, b, u, FREE + qh))
                for h in heads:
                    last = pe.matmul(pv_ps[32 * h:32 * h + 32, lo:CH], vs[u % 2][:, kt, h, :],
                                     pT[m % PRING][:, h, lo:CH], start=n == first_of[qh], stop=True,
                                     skip_group_check=True)
                if heads[-1] == GH - 1:
                    last.then_inc(weighed, 1)

            def through_bank(b, what, turns):
                if not isinstance(turns, int) or turns:
                    pe.wait_ge(turn_read, turns)
                if what[0] == "max":
                    pe.wait_ge(max_joined, count(1, b, what[1], 1))
                    pe.transpose(t_ps[0:GH * QT, 0:P], negm[:, :], ident).then_inc(max_turned, 1)
                    return
                pe.wait_ge(evacuated, count(QH, b, what[1], FREE + what[2] + 1))
                for t in range(CT):
                    last = pe.transpose(t_ps[:, t * P:(t + 1) * P], outT[:, t * P:(t + 1) * P], ident)
                last.then_inc(turned, 1)

            def batch(b, last):
                units_at, turns_at = batch_schedule(last)
                turns = 1
                for m in range(NG * NS + WLAG + 1):
                    if m < NG * NS and m % NS == 0:
                        pe.wait_ge(max_rows[m // NS], 16 * (b + 1))
                    for i, (kind, step, n) in enumerate(pieces[m] if m < len(pieces) else ()):
                        if kind == "key":
                            key_scores(b, step, n)
                        else:
                            weigh(b, step, range(n, n + WEIGH))
                        for r, k in units_at[m][i]:
                            if k == 0:
                                pe.wait_ge(loaded[r % NG], LOADS * (b + r // NG + 1))
                            score(b, r, k, k % SRING, since_last(k, NU, SRING))
                    for what in turns_at[m]:
                        through_bank(b, what, TURNS * b + turns)
                        turns = turns + 1

            pe.wait_ge(loaded[0], LOADS)
            for k in range(NU):
                score(0, 0, k, k % FIRST_RING, FIRST_RING)
            pe.wait_ge(loaded[1], LOADS)
            for k in range(LEAD):
                score(0, 1, k, k % SRING, since_last(k, NU, SRING))
                if k == 3:
                    through_bank(0, ("max", 0), 0)
            pe.wait_ge(reduced, NU)
            with pe.Fori(0, B - 1) as b:
                batch(b, False)
            batch(B - 1, True)


class Norm:

    def __init__(self, ctx, nc, taken, name, roots):
        def sb(n, shape):
            return ctx.enter_context(nc.sbuf_tensor(f"{name}_{n}", shape, F32))

        sem = stage_semaphores(nc, ctx, name, taken)

        self.eps, self.neg_half = roots
        self.bst, self.mv = sb("bst", [P, NCH, CT, 6]), sb("mv", [P, NCH, CT, 2])
        self.ve, self.rs = sb("ve", [P, NCH, CT]), sb("rs", [P, NCH, CT])
        self.stats_in, self.mean_var, self.eps_added, self.rooted, self.done = (
            sem(n) for n in ("stats_in", "mean_var", "eps_added", "rooted", "done"))

    def on_vector(self, dve, n0, before, src, dst):
        def stats(c):
            for t in range(CT):
                last = dve.bn_stats(self.bst[:, c, t, :], src(c)[:, t, :])
            last.then_inc(self.stats_in, 1)

        def mean(c):
            for t in range(CT):
                last = dve.bn_aggr(self.mv[:, c, t, :], self.bst[:, c, t, :])
            last.then_inc(self.mean_var, 1)

        def scale(c):
            dve.wait_ge(self.rooted, n0 + c + 1)
            for t in range(CT):
                last = dve.tensor_scalar(dst(c)[:, t, :], src(c)[:, t, :], self.mv[:, c, t, 0:1],
                                         self.rs[:, c, t:t + 1], ALU.subtract, ALU.mult)
            last.then_inc(self.done, 1)

        for c in range(NCH):
            if c >= 2:
                dve.wait_ge(self.stats_in, n0 + c - 1)
            before(c)
            stats(c)
            if c >= 2:
                mean(c - 2)
        for c in range(NCH):
            if c < 2:
                dve.wait_ge(self.stats_in, n0 + NCH - 1 + c)
            scale(c)
            if c < 2:
                mean(NCH - 2 + c)

    def root(self, pool, n, c):
        pool.wait_ge(self.mean_var, n + 1)
        pool.tensor_tensor(self.ve[:, c, :], self.mv[:, c, :, 1], self.eps[:, 0:CT], ALU.add)\
            .then_inc(self.eps_added, 1)
        pool.wait_ge(self.eps_added, n + 1)
        pool.tensor_tensor(self.rs[:, c, :], self.ve[:, c, :], self.neg_half[:, 0:CT], ALU.pow)\
            .then_inc(self.rooted, 1)


def turn(pe, bank, src, ident):
    for t in range(CT):
        last = pe.transpose(bank[:, t * P:(t + 1) * P], src[:, t * P:(t + 1) * P], ident)
    return last


def tokens_out(pe, bank, src, weight):
    for t in range(CT):
        last = pe.matmul(bank[:, t * P:(t + 1) * P], src[:, t * P:(t + 1) * P], weight, start=True, stop=True)
    return last


class Qkv:

    def __init__(self, ctx, nc, taken, name, wq, wk, wv, bq, bk, bv, scr, slots, loaded, written, v_tm, x32, part):
        sem = stage_semaphores(nc, ctx, name, taken)

        self.w, self.wv = (wq, wk), wv
        self.b, self.bv, self.scr, self.v_tm, self.x32 = (bq, bk), bv, scr, v_tm, x32
        self.part, self.slots, self.loaded, self.written = part, slots, loaded, written
        self.mm = [sem("q_mm"), sem("k_mm")]
        self.ev = [sem("q_ev"), sem("k_ev")]
        self.first = [sem("q_first"), sem("k_first")]
        self.rest1 = [sem("q_rest1"), sem("k_rest1")]
        self.second = [sem("q_second"), sem("k_second")]
        self.parted = [sem("q_parted"), sem("k_parted")]
        self.v_mm, self.v_ev = sem("v_mm"), sem("v_ev")

    def pe(self, pe, it, ready, src, bank):
        for s in range(2):
            for c in range(NCH):
                n = NCH * it + c
                if s == 0:
                    pe.wait_ge(ready, n + 1)
                if s == 0:
                    pe.wait_ge(self.v_ev, FREE + NCH * it)
                pe.matmul(bank[4 + c if s == 0 else c], self.w[s], src[:, c, :], start=True, stop=True)\
                    .then_inc(self.mm[s], 1)
        for c in range(NCH):
            pe.wait_ge(self.ev[0], FREE + NCH * it + c + 1)
            tokens_out(pe, bank[4 + c], src[:, c, :], self.wv).then_inc(self.v_mm, 1)

    def act(self, act, it, bank):
        for s in range(2):
            for c in range(NCH):
                n = NCH * it + c
                act.wait_ge(self.mm[s], n + 1)
                act.wait_ge(self.parted[s], FREE + NCH * it)
                act.activation(self.x32[s][:, c, :], bank[4 + c if s == 0 else c], ACT.Identity, bias=self.b[s])\
                    .then_inc(self.ev[s], 1)
        for s in range(2):
            for c in range(NCH):
                act.wait_ge(self.ev[s], FREE + NCH * it + c + 1)
                act.wait_ge(self.written[c], FREE + 2 * 16 * it)
                act.activation(self.part[s][:, c, 0, :], self.x32[s][:, c, :], ACT.Copy)\
                    .then_inc(self.first[s], 1)
        for s in range(2):
            for c in range(NCH):
                act.wait_ge(self.rest1[s], NCH * it + c + 1)
                act.activation(self.part[s][:, c, 1, :], self.x32[s][:, c, :], ACT.Copy)\
                    .then_inc(self.second[s], 1)

    def rest(self, eng, s, it):
        for c in range(NCH):
            eng.wait_ge(self.first[s], NCH * it + c + 1)
            eng.tensor_tensor(self.x32[s][:, c, :], self.x32[s][:, c, :], self.part[s][:, c, 0, :], ALU.subtract)\
                .then_inc(self.rest1[s], 1)
        for c in range(NCH):
            eng.wait_ge(self.second[s], NCH * it + c + 1)
            eng.tensor_tensor(self.part[s][:, c, 2, :], self.x32[s][:, c, :], self.part[s][:, c, 1, :],
                              ALU.subtract).then_inc(self.parted[s], 1)

    def values(self, dve, it, bank):
        for c in range(NCH):
            dve.wait_ge(self.v_mm, NCH * it + c + 1)
            dve.tensor_tensor(self.v_tm[:, chunk_tiles(it, c), :], bank[4 + c].rearrange("p (t f) -> p t f", f=P),
                              self.bv.unsqueeze(1).to_broadcast([P, CT, P]), ALU.add).then_inc(self.v_ev, 1)

    def write(self, sp, it):
        for c in range(NCH):
            for s in range(2):
                sp.wait_ge(self.parted[s], FREE + NCH * it + c + 1)
                dst = self.scr[s][:, :, bass.ds((it * NCH + c) * CH, CH)]
                sp.dma_start(dst.rearrange("(j d) h t -> (d h) j t", d=HD), self.part[s][:, c, :, :])\
                    .then_inc(self.written[c], 16)

    def on_sync(self, sp):
        for c in range(NCH):
            sp.sem_inc(self.written[c], FREE)
        with sp.Fori(0, NLOOP - 1) as it:
            self.write(sp, it)
        for c in range(SEQ // CH):
            sp.wait_ge(self.written[c], FREE + 2 * 16 * (NLOOP - 1))
        for u in range(NG - 1):
            load_group(sp, self.scr, self.slots, self.loaded, 0, u)
        self.write(sp, NLOOP - 1)


def rows(t):
    return t.rearrange("p (t f) -> p t f", f=P)


def banks(ps):
    return [ps[:, n * BANK:(n + 1) * BANK] for n in range(8)]


def first_stage(nc, taken, W, C, R, scr, slots, loaded, written, x_in, x_tm, v_tm, ident, roots):
    with ExitStack() as ctx:
        def sb(n, shape=(P, NCH, CH), dt=F32):
            return ctx.enter_context(nc.sbuf_tensor(f"a_{n}", list(shape), dt))

        sem = stage_semaphores(nc, ctx, "a", taken)

        part = [sb(f"part{i}", (P, NCH, PARTS, CH), BF16) for i in range(2)]
        n_tm, xT, q32, k32 = sb("n_tm"), sb("xT"), sb("q32"), sb("k32")
        bank = banks(ctx.enter_context(nc.psum_tensor("a_ps", [P, 8 * BANK], F32)))
        ln = Norm(ctx, nc, taken, "a_ln", roots)
        qkv = Qkv(ctx, nc, taken, "a_qkv", W("q0"), W("k0"), W("v0"), C("bq0"), C("bk0"), R("bv0"),
                  scr, slots, loaded, written, v_tm, (q32, k32), part)
        n_turned, x_ready = sem("n_turned"), sem("x_ready")
        block = ctx.enter_context(nc.Block())

        @block.sync
        def _(sp):
            qkv.on_sync(sp)

        @block.gpsimd
        def _(pool):
            pool.sem_inc(qkv.parted[1], FREE)
            with pool.Fori(0, NLOOP) as it:
                for c in range(NCH):
                    ln.root(pool, NCH * it + c, c)
                qkv.rest(pool, 1, it)

        @block.scalar
        def _(act):
            act.sem_inc(qkv.ev[0], FREE)
            act.sem_inc(qkv.ev[1], FREE)
            with act.Fori(0, NLOOP) as it:
                for c in range(NCH):
                    act.wait_ge(n_turned, NCH * it + c + 1)
                    act.activation(xT[:, c, :], bank[c], ACT.Identity, bias=C("b_attn"), scale=C("g_attn"))\
                        .then_inc(x_ready, 1)
                qkv.act(act, it, bank)

        @block.vector
        def _(dve):
            dve.sem_inc(qkv.v_ev, FREE)
            dve.sem_inc(qkv.parted[0], FREE)
            with dve.Fori(0, NLOOP) as it:
                def before(c):
                    dve.wait_ge(x_in[c * CH // SEQ], 16 * (it + 1))

                ln.on_vector(dve, NCH * it, before, lambda c: x_tm[:, chunk_tiles(it, c), :],
                             lambda c: rows(n_tm[:, c, :]))
                qkv.values(dve, it, bank)
                qkv.rest(dve, 0, it)

        @block.tensor
        def _(pe):
            with pe.Fori(0, NLOOP) as it:
                for c in range(NCH):
                    pe.wait_ge(ln.done, NCH * it + c + 1)
                    pe.wait_ge(qkv.ev[1], FREE + NCH * it)
                    turn(pe, bank[c], n_tm[:, c, :], ident).then_inc(n_turned, 1)
                qkv.pe(pe, it, x_ready, xT, bank)


def middle_stage(nc, taken, W, C, R, scr, slots, loaded, written, x_tm, v_tm, attn_tm, ident, roots,
                 wx_step, w_lin):
    with ExitStack() as ctx:
        def sb(n, shape=(P, NCH, CH), dt=F32):
            return ctx.enter_context(nc.sbuf_tensor(f"m_{n}", list(shape), dt))

        sem = stage_semaphores(nc, ctx, "m", taken)

        three = ctx.enter_context(nc.sbuf_tensor("m_n_x2_xx", [P, 3, NCH, CH], F32))
        n_tm = three[:, 0, :, :]
        x2 = y2p = three[:, 1, :, :]
        xx = three[:, 2, :, :]
        parts = three[:, :, :, :].rearrange("p a c t -> p (a c t)").bitcast(BF16)
        parts = parts.rearrange("p (s c j t) -> p s c j t", s=2, c=NCH, j=PARTS)
        part = [parts[:, s, :, :, :] for s in range(2)]
        both = ctx.enter_context(nc.sbuf_tensor("m_u_t", [P, 2, NCH, CH], F32))
        at = u = both[:, 0, :, :]
        aT = t = both[:, 1, :, :]
        hh = [both[:, i, :, :] for i in range(2)]
        cT = hT = sb("cT_hT")
        x1 = x3 = sb("x1_x3")
        xs = y1 = sb("xs_y1")
        w = y2 = sb("w_y2")
        bank = banks(ctx.enter_context(nc.psum_tensor("m_ps", [P, 8 * BANK], F32)))
        ln1, ln2, ln3, ln4 = (Norm(ctx, nc, taken, f"m_ln{i}", roots) for i in range(1, 5))
        qkv = Qkv(ctx, nc, taken, "m_qkv", W("q1"), W("k1"), W("v1"), C("bq1"), C("bk1"), R("bv1"),
                  scr, slots, loaded, written, v_tm, (hh[0], hh[1]), part)
        (at_ready, at_turned, aT_ready, c_mm, cT_ready, c_turned, x1_ready, n1_turned, xs_ready, z_ready,
         tanhed, lagged, sped, moved, xs_turned, xb_ready, x2_ready, xx_ready, n2_turned, hT_ready, f_mm, gelued,
         o_mm, x3_ready, y1_turned, y1T_ready, lin_mm, y2p_ready, y2_turned, y2T_ready, y2_kept) = (sem(n) for n in (
             "at_ready at_turned aT_ready c_mm cT_ready c_turned x1_ready n1_turned xs_ready z_ready tanhed lagged "
             "sped moved xs_turned xb_ready x2_ready xx_ready n2_turned hT_ready f_mm gelued o_mm x3_ready y1_turned "
             "y1T_ready lin_mm y2p_ready y2_turned y2T_ready y2_kept").split())
        block = ctx.enter_context(nc.Block())

        @block.sync
        def _(sp):
            qkv.on_sync(sp)

        @block.gpsimd
        def _(pool):
            pool.sem_inc(qkv.parted[1], FREE)
            with pool.Fori(0, NLOOP) as it:
                n0 = NCH * it
                for c in range(NCH):
                    ln1.root(pool, n0 + c, c)
                for c in range(NCH):
                    pool.wait_ge(written[c], FREE + 2 * 16 * it)
                for c in range(NCH):
                    pool.tensor_tensor(rows(xx[:, c, :]), x_tm[:, chunk_tiles(it, c), :],
                                       R("fb2").unsqueeze(1).to_broadcast([P, CT, P]), ALU.add)\
                        .then_inc(xb_ready, 1)
                for k in range(ITERS):
                    for c in range(NCH):
                        m = (ITERS * it + k) * NCH + c
                        pool.wait_ge(tanhed, m + 1)
                        if k:
                            pool.wait_ge(moved, m - NCH + 1)
                        pool.tensor_tensor((t if k else w)[:, c, :], u[:, c, :], xs[:, c, :], ALU.subtract)\
                            .then_inc(lagged, 1)
                for c in range(NCH):
                    pool.wait_ge(x2_ready, n0 + c + 1)
                    pool.wait_ge(xb_ready, n0 + c + 1)
                    pool.tensor_tensor(xx[:, c, :], xx[:, c, :], x2[:, c, :], ALU.add).then_inc(xx_ready, 1)
                for c in range(NCH):
                    ln2.root(pool, n0 + c, c)
                for c in range(NCH):
                    ln3.root(pool, n0 + c, c)
                for c in range(NCH):
                    ln4.root(pool, n0 + c, c)
                qkv.rest(pool, 1, it)

        @block.scalar
        def _(act):
            act.sem_inc(qkv.ev[0], FREE)
            act.sem_inc(qkv.ev[1], FREE)
            with act.Fori(0, NLOOP) as it:
                n0 = NCH * it
                for c in range(NCH):
                    act.wait_ge(qkv.parted[0], FREE + n0)
                    act.activation(rows(at[:, c, :]), attn_tm[:, chunk_tiles(it, c), :], ACT.Copy)\
                        .then_inc(at_ready, 1)
                for c in range(NCH):
                    act.wait_ge(at_turned, n0 + c + 1)
                    act.wait_ge(qkv.parted[1], FREE + n0)
                    act.activation(aT[:, c, :], bank[c], ACT.Copy).then_inc(aT_ready, 1)
                for c in range(NCH):
                    act.wait_ge(c_mm, n0 + c + 1)
                    act.activation(cT[:, c, :], bank[4 + c], ACT.Identity, bias=C("bo0")).then_inc(cT_ready, 1)
                for c in range(NCH):
                    act.wait_ge(n1_turned, n0 + c + 1)
                    act.activation(xs[:, c, :], bank[4 + c], ACT.Identity, bias=C("b1"), scale=C("g1"))\
                        .then_inc(xs_ready, 1)
                for k in range(ITERS):
                    for c in range(NCH):
                        m = (ITERS * it + k) * NCH + c
                        act.wait_ge(z_ready, m + 1)
                        act.activation(u[:, c, :], bank[c], ACT.Tanh, bias=C("b_inl")).then_inc(tanhed, 1)
                for c in range(NCH):
                    act.wait_ge(n2_turned, n0 + c + 1)
                    act.activation(hT[:, c, :], bank[c], ACT.Identity, bias=C("b2"), scale=C("g2"))\
                        .then_inc(hT_ready, 1)
                for c in range(NCH):
                    for j in range(4):
                        act.wait_ge(f_mm, 4 * (n0 + c) + j + 1)
                        if c >= 2:
                            act.wait_ge(o_mm, n0 + c - 1)
                        act.activation(hh[c % 2][:, j, :], bank[4 + j], ACT.Gelu, bias=C(f"f{j}"))\
                            .then_inc(gelued, 1)
                for c in range(NCH):
                    act.wait_ge(y1_turned, n0 + c + 1)
                    act.activation(hT[:, c, :], bank[4 + c], ACT.Copy).then_inc(y1T_ready, 1)
                for c in range(NCH):
                    act.wait_ge(y2_turned, n0 + c + 1)
                    act.activation(hT[:, c, :], bank[4 + c], ACT.Copy).then_inc(y2T_ready, 1)
                    act.activation(x_tm[:, chunk_tiles(it, c), :], rows(y2[:, c, :]), ACT.Copy).then_inc(y2_kept, 1)
                act.wait_ge(ln4.done, n0 + NCH)
                qkv.act(act, it, bank)

        @block.vector
        def _(dve):
            def norm(ln, n0, before, src, dst):
                ln.on_vector(dve, n0, before, lambda c: rows(src[:, c, :]), lambda c: rows(dst[:, c, :]))

            dve.sem_inc(qkv.v_ev, FREE)
            dve.sem_inc(qkv.parted[0], FREE)
            with dve.Fori(0, NLOOP) as it:
                n0 = NCH * it
                def before_ln1(c):
                    dve.wait_ge(c_turned, n0 + c + 1)
                    dve.tensor_tensor(rows(x1[:, c, :]), rows(bank[c]), x_tm[:, chunk_tiles(it, c), :], ALU.add)\
                        .then_inc(x1_ready, 1)
                    dve.wait_ge(x1_ready, n0 + c + 1)

                for c in range(NCH):
                    dve.wait_ge(written[c], FREE + 2 * 16 * it)
                norm(ln1, n0, before_ln1, x1, n_tm)
                for k in range(ITERS):
                    for c in range(NCH):
                        m = (ITERS * it + k) * NCH + c
                        dve.wait_ge(lagged, m + 1)
                        if k:
                            dve.scalar_tensor_tensor(out=w[:, c, :], in0=w[:, c, :], scalar=1.0 - DT, in1=t[:, c, :],
                                                     op0=ALU.mult, op1=ALU.add).then_inc(sped, 1)
                            dve.wait_ge(sped, ((ITERS - 1) * it + k - 1) * NCH + c + 1)
                        dve.scalar_tensor_tensor(out=xs[:, c, :], in0=w[:, c, :], scalar=DT * DT, in1=xs[:, c, :],
                                                 op0=ALU.mult, op1=ALU.add).then_inc(moved, 1)
                def before_ln2(c):
                    dve.wait_ge(xs_turned, n0 + c + 1)
                    dve.tensor_tensor(x2[:, c, :], bank[4 + c], x1[:, c, :], ALU.add).then_inc(x2_ready, 1)
                    dve.wait_ge(x2_ready, n0 + c + 1)

                norm(ln2, n0, before_ln2, x2, n_tm)
                def before_ln3(c):
                    dve.wait_ge(o_mm, n0 + c + 1)
                    dve.wait_ge(xx_ready, n0 + c + 1)
                    dve.tensor_tensor(x3[:, c, :], bank[c], xx[:, c, :], ALU.add).then_inc(x3_ready, 1)
                    dve.wait_ge(x3_ready, n0 + c + 1)

                norm(ln3, n0, before_ln3, x3, y1)
                def before_ln4(c):
                    dve.wait_ge(lin_mm, n0 + c + 1)
                    dve.tensor_tensor(y2p[:, c, :], bank[c], y1[:, c, :], ALU.add).then_inc(y2p_ready, 1)
                    dve.wait_ge(y2p_ready, n0 + c + 1)

                norm(ln4, n0, before_ln4, y2p, y2)
                qkv.values(dve, it, bank)
                qkv.rest(dve, 0, it)

        @block.tensor
        def _(pe):
            with pe.Fori(0, NLOOP) as it:
                n0 = NCH * it
                for c in range(NCH):
                    pe.wait_ge(at_ready, n0 + c + 1)
                    pe.wait_ge(qkv.ev[1], FREE + n0)
                    turn(pe, bank[c], at[:, c, :], ident).then_inc(at_turned, 1)
                for c in range(NCH):
                    pe.wait_ge(aT_ready, n0 + c + 1)
                    pe.wait_ge(qkv.v_ev, FREE + n0)
                    pe.matmul(bank[4 + c], W("o0"), aT[:, c, :], start=True, stop=True).then_inc(c_mm, 1)
                for c in range(NCH):
                    pe.wait_ge(cT_ready, n0 + c + 1)
                    turn(pe, bank[c], cT[:, c, :], ident).then_inc(c_turned, 1)
                for c in range(NCH):
                    pe.wait_ge(ln1.done, n0 + c + 1)
                    turn(pe, bank[4 + c], n_tm[:, c, :], ident).then_inc(n1_turned, 1)
                for c in range(NCH):
                    pe.wait_ge(xs_ready, n0 + c + 1)
                    pe.matmul(bank[c], W("ctx"), cT[:, c, :], start=True, stop=False)
                    pe.matmul(bank[c], W("x"), xs[:, c, :], start=False, stop=True).then_inc(z_ready, 1)
                for k in range(ITERS - 1):
                    for c in range(NCH):
                        if k:
                            pe.wait_ge(sped, ((ITERS - 1) * it + k - 1) * NCH + c + 1)
                        else:
                            pe.wait_ge(lagged, ITERS * n0 + c + 1)
                        pe.matmul(bank[c], wx_step, w[:, c, :], start=False, stop=True, skip_group_check=True)\
                            .then_inc(z_ready, 1)
                for c in range(NCH):
                    pe.wait_ge(moved, (ITERS * it + ITERS - 1) * NCH + c + 1)
                    turn(pe, bank[4 + c], xs[:, c, :], ident).then_inc(xs_turned, 1)
                for c in range(NCH):
                    pe.wait_ge(ln2.done, n0 + c + 1)
                    turn(pe, bank[c], n_tm[:, c, :], ident).then_inc(n2_turned, 1)

                def down(c):
                    pe.wait_ge(gelued, 4 * (n0 + c) + 4)
                    for i in range(CT):
                        for j in range(4):
                            last = pe.matmul(bank[c][:, i * P:(i + 1) * P], hh[c % 2][:, j, i * P:(i + 1) * P],
                                             W("f2")[:, j * P:(j + 1) * P], start=j == 0, stop=j == 3)
                    last.then_inc(o_mm, 1)

                pe.wait_ge(x2_ready, n0 + NCH)
                for c in range(NCH):
                    pe.wait_ge(hT_ready, n0 + c + 1)
                    for j in range(4):
                        if c:
                            pe.wait_ge(gelued, 4 * (n0 + c - 1) + j + 1)
                        pe.matmul(bank[4 + j], W("f1")[:, j * P:(j + 1) * P], hT[:, c, :], start=True, stop=True)\
                            .then_inc(f_mm, 1)
                    if c:
                        down(c - 1)
                down(NCH - 1)
                for c in range(NCH):
                    pe.wait_ge(ln3.done, n0 + c + 1)
                    turn(pe, bank[4 + c], y1[:, c, :], ident).then_inc(y1_turned, 1)
                for c in range(NCH):
                    pe.wait_ge(y1T_ready, n0 + c + 1)
                    tokens_out(pe, bank[c], hT[:, c, :], w_lin).then_inc(lin_mm, 1)
                for c in range(NCH):
                    pe.wait_ge(ln4.done, n0 + c + 1)
                    turn(pe, bank[4 + c], y2[:, c, :], ident).then_inc(y2_turned, 1)
                qkv.pe(pe, it, y2T_ready, hT, bank)


def last_stage(nc, taken, W, C, R, out, x_tm, attn_tm, ident, roots):
    with ExitStack() as ctx:
        def sb(n, shape=(P, NCH, CH), dt=F32):
            return ctx.enter_context(nc.sbuf_tensor(f"e_{n}", list(shape), dt))

        sem = stage_semaphores(nc, ctx, "e", taken)

        xb, x1, y3, yb, hT, x4, y4 = (sb(n) for n in "xb x1 y3 yb hT x4 y4".split())
        at, aT = hh = sb("at_hh0"), sb("aT_hh1")
        bank = banks(ctx.enter_context(nc.psum_tensor("e_ps", [P, 8 * BANK], F32)))
        ln5, ln6 = (Norm(ctx, nc, taken, f"e_ln{i}", roots) for i in (5, 6))
        (at_ready, at_turned, aT_ready, o_mm, xb_ready, x1_ready, yb_ready, y3_turned, hT_ready, f_mm, relued, d_mm,
         x4_ready) = (sem(n) for n in ("at_ready at_turned aT_ready o_mm xb_ready x1_ready yb_ready y3_turned "
                                       "hT_ready f_mm relued d_mm x4_ready").split())
        stored = [sem(f"stored{c}") for c in range(NCH)]
        block = ctx.enter_context(nc.Block())

        @block.sync
        def _(sp):
            for c in range(NCH):
                sp.sem_inc(stored[c], FREE)
            with sp.Fori(0, NLOOP) as it:
                for c in range(NCH):
                    sp.wait_ge(ln6.done, NCH * it + c + 1)
                    sp.dma_start(out.rearrange("b (n p) d -> p (b n) d", p=P)[:, chunk_tiles(it, c), :],
                                 rows(y4[:, c, :])).then_inc(stored[c], 16)
            for c in range(NCH):
                sp.wait_ge(stored[c], FREE + 16 * NLOOP)

        @block.gpsimd
        def _(pool):
            with pool.Fori(0, NLOOP) as it:
                n0 = NCH * it
                for c in range(NCH):
                    pool.tensor_tensor(rows(xb[:, c, :]), x_tm[:, chunk_tiles(it, c), :],
                                       R("bo1").unsqueeze(1).to_broadcast([P, CT, P]), ALU.add)\
                        .then_inc(xb_ready, 1)
                for c in range(NCH):
                    ln5.root(pool, n0 + c, c)
                for c in range(NCH):
                    pool.wait_ge(ln5.done, n0 + c + 1)
                    pool.tensor_tensor(rows(yb[:, c, :]), rows(y3[:, c, :]),
                                       R("hb2").unsqueeze(1).to_broadcast([P, CT, P]), ALU.add)\
                        .then_inc(yb_ready, 1)
                for c in range(NCH):
                    ln6.root(pool, n0 + c, c)

        @block.scalar
        def _(act):
            act.sem_inc(relued, FREE)
            with act.Fori(0, NLOOP) as it:
                n0 = NCH * it
                for c in range(NCH):
                    act.wait_ge(d_mm, FREE + n0)
                    act.activation(rows(at[:, c, :]), attn_tm[:, chunk_tiles(it, c), :], ACT.Copy)\
                        .then_inc(at_ready, 1)
                for c in range(NCH):
                    act.wait_ge(at_turned, n0 + c + 1)
                    act.activation(aT[:, c, :], bank[c], ACT.Copy).then_inc(aT_ready, 1)
                for c in range(NCH):
                    act.wait_ge(y3_turned, n0 + c + 1)
                    act.activation(hT[:, c, :], bank[c], ACT.Copy).then_inc(hT_ready, 1)
                for c in range(NCH):
                    for j in range(4):
                        act.wait_ge(f_mm, 4 * (n0 + c) + j + 1)
                        if c >= 2:
                            act.wait_ge(d_mm, FREE + n0 + c - 1)
                        act.activation(hh[c % 2][:, j, :], bank[4 + j], ACT.Relu, bias=C(f"h{j}"))\
                            .then_inc(relued, 1)

        @block.vector
        def _(dve):
            def norm(ln, n0, before, src, dst):
                ln.on_vector(dve, n0, before, lambda c: rows(src[:, c, :]), lambda c: rows(dst[:, c, :]))

            dve.sem_inc(x4_ready, FREE)
            with dve.Fori(0, NLOOP) as it:
                n0 = NCH * it

                def before_ln5(c):
                    dve.wait_ge(o_mm, n0 + c + 1)
                    dve.wait_ge(xb_ready, n0 + c + 1)
                    dve.tensor_tensor(x1[:, c, :], bank[4 + c], xb[:, c, :], ALU.add).then_inc(x1_ready, 1)
                    dve.wait_ge(x1_ready, n0 + c + 1)

                norm(ln5, n0, before_ln5, x1, y3)

                def before_ln6(c):
                    dve.wait_ge(d_mm, FREE + n0 + c + 1)
                    dve.wait_ge(yb_ready, n0 + c + 1)
                    dve.tensor_tensor(x4[:, c, :], bank[c], yb[:, c, :], ALU.add).then_inc(x4_ready, 1)
                    dve.wait_ge(x4_ready, FREE + n0 + c + 1)

                for c in range(NCH):
                    dve.wait_ge(stored[c], FREE + 16 * it)
                norm(ln6, n0, before_ln6, x4, y4)

        @block.tensor
        def _(pe):
            pe.sem_inc(d_mm, FREE)
            with pe.Fori(0, NLOOP) as it:
                n0 = NCH * it
                for c in range(NCH):
                    pe.wait_ge(at_ready, n0 + c + 1)
                    pe.wait_ge(x4_ready, FREE + n0)
                    turn(pe, bank[c], at[:, c, :], ident).then_inc(at_turned, 1)
                for c in range(NCH):
                    pe.wait_ge(aT_ready, n0 + c + 1)
                    pe.wait_ge(relued, FREE + 4 * n0)
                    tokens_out(pe, bank[4 + c], aT[:, c, :], W("o1")).then_inc(o_mm, 1)
                for c in range(NCH):
                    pe.wait_ge(ln5.done, n0 + c + 1)
                    turn(pe, bank[c], y3[:, c, :], ident).then_inc(y3_turned, 1)

                def down(c):
                    pe.wait_ge(relued, FREE + 4 * (n0 + c) + 4)
                    for i in range(CT):
                        for j in range(4):
                            last = pe.matmul(bank[c][:, i * P:(i + 1) * P], hh[c % 2][:, j, i * P:(i + 1) * P],
                                             W("g2")[:, j * P:(j + 1) * P], start=j == 0, stop=j == 3)
                    last.then_inc(d_mm, 1)

                pe.wait_ge(x1_ready, n0 + NCH)
                for c in range(NCH):
                    pe.wait_ge(hT_ready, n0 + c + 1)
                    for j in range(4):
                        if c:
                            pe.wait_ge(relued, FREE + 4 * (n0 + c - 1) + j + 1)
                        pe.matmul(bank[4 + j], W("g1")[:, j * P:(j + 1) * P], hT[:, c, :], start=True, stop=True)\
                            .then_inc(f_mm, 1)
                    if c:
                        down(c - 1)
                down(NCH - 1)


def two_layer_kernel(nc, x, w_pack, c_pack, r_pack, out):
    scr = [nc.dram_tensor(f"scr_{n}", [PARTS * HD, H, TOK], BF16, kind="Internal").ap() for n in ("q0", "k0", "q1", "k1")]
    scr_m = [nc.dram_tensor(f"scr_m{i}", [3, B * H * QT, P], BF16, kind="Internal").ap() for i in range(2)]
    with ExitStack() as ctx:
        def sb(n, shape, dt=F32):
            return ctx.enter_context(nc.sbuf_tensor(n, shape, dt))

        def sem(n):
            return ctx.enter_context(nc.semaphore(n))

        def words(t):
            return t.rearrange("p h t -> p (h t)").bitcast(F32)

        x_tm = sb("x_tm", [P, TILES, D])
        v_tm = sb("v_tm", [P, TILES, D])
        attn_tm = sb("attn_tm", [P, TILES, D])
        w_sb = sb("w_sb", [P, W_COLS])
        c_sb = sb("c_sb", [P, len(C_AT)])
        r_sb = sb("r_sb", [P, len(R_AT), D])
        slots = [[sb(f"{side}s{u}", [P, GH, SEQ], BF16) for u in range(NG)] for side in "QK"]
        wx_step = sb("wx_step", [P, D])
        w_lin = sb("w_lin", [P, D])
        ident = sb("ident", [P, P])
        ident_bf = sb("ident_bf", [P, P], BF16)
        mask_neg = sb("mask_neg", [P, P], BF16)
        roots = [sb("eps", [P, CT]), sb("neg_half", [P, CT])]

        def W(n):
            at, width = W_AT[n]
            return w_sb[:, at:at + width]

        def C(n):
            return c_sb[:, C_AT[n]:C_AT[n] + 1]

        def R(n):
            return r_sb[:, R_AT[n], :]

        w_first_in, w_in, small_in, blank, cut_out = (sem(n) for n in (
            "w_first_in w_in small_in blank cut_out").split())
        x_in = [sem(f"x_in{i}") for i in range(B // NLOOP)]
        loaded = [[sem(f"loaded{layer}_{u}") for u in range(NG)] for layer in range(2)]
        written = [[sem(f"written{layer}_{c}") for c in range(NCH)] for layer in range(2)]
        W_FIRST = 3 * D

        with nc.Block() as block:
            @block.sync
            def _(sp):
                for b in range(B):
                    if b >= len(x_in):
                        sp.wait_ge(x_in[b % len(x_in)], 16 * (b // len(x_in)))
                    sp.dma_start(x_tm[:, b * QT:(b + 1) * QT, :],
                                 x[b, :, :].rearrange("(n p) d -> p n d", p=P)).then_inc(x_in[b % len(x_in)], 16)
                sp.dma_start(w_sb[:, W_FIRST:], w_pack[:, W_FIRST:]).then_inc(w_in, 16)

            @block.scalar
            def _(act):
                act.dma_start(c_sb[:, :], c_pack).then_inc(small_in, 16)
                act.dma_start(w_sb[:, 0:W_FIRST], w_pack[:, 0:W_FIRST]).then_inc(w_first_in, 16)
                act.dma_start(r_sb[:, :, :], r_pack.unsqueeze(0).to_broadcast([P, len(R_AT), D]))\
                    .then_inc(small_in, 16)
                act.wait_ge(w_first_in, 16)
                act.wait_ge(small_in, 32)

            @block.gpsimd
            def _(pool):
                pool.memset(ident[:, :], 0.0).then_inc(blank, 1)
                pool.memset(mask_neg[:, :], 0.0).then_inc(blank, 1)
                pool.memset(roots[0][:, :], EPS)
                pool.memset(roots[1][:, :], -0.5)
                pool.wait_ge(blank, 2)
                pool.affine_select(out=ident[:, :], in_=ident[:, :], compare_op=ALU.not_equal, fill=1.0, base=0,
                                   pattern=[[-1, P]], channel_multiplier=1).then_inc(cut_out, 1)
                pool.affine_select(out=mask_neg[:, :], in_=mask_neg[:, :], compare_op=ALU.is_ge, fill=-3.0e38, base=0,
                                   pattern=[[-1, P]], channel_multiplier=1).then_inc(cut_out, 1)
                for u in range(NG):
                    pool.memset(words(slots[0][u][:, :, :]), 0.0)

            @block.vector
            def _(dve):
                for u in range(NG):
                    dve.memset(words(slots[1][u][:, :, :]), BF16_ONES)
                dve.wait_ge(cut_out, 1)
                dve.tensor_copy(ident_bf[:, :], ident[:, :])

        taken = []
        first_stage(nc, taken, W, C, R, scr[0:2], slots, loaded[0], written[0], x_in, x_tm, v_tm, ident[:, :], roots)
        attention(nc, taken, "l0", True, scr[0:2], scr_m[0], slots, loaded[0], written[0], v_tm, attn_tm,
                  ident[:, :], mask_neg[:, :], ident_bf[:, :])
        retire(nc, taken)
        with nc.Block() as block:
            @block.vector
            def _(dve):
                dve.wait_ge(w_in, 16)
                dve.tensor_scalar(wx_step[:, :], W("x"), DT * DT, None, ALU.mult)
                dve.tensor_tensor(w_lin[:, :], W("lin"), W("dis"), ALU.add)

        middle_stage(nc, [], W, C, R, scr[2:4], slots, loaded[1], written[1], x_tm, v_tm, attn_tm, ident[:, :],
                     roots, wx_step[:, :], w_lin[:, :])
        attention(nc, [], "l1", False, scr[2:4], scr_m[1], slots, loaded[1], written[1], v_tm, attn_tm,
                  ident[:, :], mask_neg[:, :], ident_bf[:, :])
        last_stage(nc, [], W, C, R, out, x_tm, attn_tm, ident[:, :], roots)


def kernel(**inputs):
    import numpy as np
    import concourse.bacc as bacc
    from concourse import mybir as mb
    from concourse.bass_utils import run_bass_kernel_spmd

    a = {n: np.asarray(v) for n, v in inputs.items()}

    def by_dim(w):
        return w.reshape(w.shape[:-1] + (H, HD)).swapaxes(-1, -2).reshape(w.shape)

    def parts0(w):
        q, k, v = (w[..., n * D:(n + 1) * D] for n in range(3))
        return by_dim(q), by_dim(k), v

    def parts1(w):
        w = w.reshape(w.shape[:-1] + (H, 3, HD))
        q, k, v = (w[..., n, :].reshape(w.shape[:-3] + (D,)) for n in range(3))
        return by_dim(q), by_dim(k), v

    def by_rows(w):
        return w.reshape(4, P, D).transpose(1, 0, 2).reshape(P, 4 * D)

    disha = a["L0_ffn_disha"]
    w_pack = np.concatenate([
        *parts0(a["L0_attn_qkv_w"]), a["L0_attn_out_w"], a["L0_attn_w_ctx"], a["L0_attn_w_x"], a["L0_attn_ff_w1"],
        by_rows(a["L0_attn_ff_w2"]), a["L0_ffn_weight"].T, np.concatenate([disha, disha], axis=0),
        *parts1(a["L1_attn_Wqkv"]), a["L1_attn_Wout"], a["L1_ffn_W1"], by_rows(a["L1_ffn_W2"])], axis=1)
    bq0, bk0, bv0 = parts0(a["L0_attn_qkv_b"])
    bq1, bk1, bv1 = parts1(a["L1_attn_bqkv"])
    c_pack = np.stack([
        bq0, bk0, a["L0_attn_out_b"], a["L0_attn_g_attn"], a["L0_attn_b_attn"], a["L0_attn_g1"], a["L0_attn_b1"],
        a["L0_attn_g2"], a["L0_attn_b2"], a["L0_attn_b_inl"], *a["L0_attn_ff_b1"].reshape(4, P),
        bq1, bk1, *a["L1_ffn_b1"].reshape(4, P)], axis=1)
    r_pack = np.stack([bv0, a["L0_attn_ff_b2"], bv1, a["L1_attn_bout"], a["L1_ffn_b2"]])

    nc = bacc.Bacc("TRN2", target_bir_lowering=False, num_devices=1)
    arrays, args = {}, []
    for name, v in (("x", a["L0_attn_x"]), ("w_pack", w_pack), ("c_pack", c_pack), ("r_pack", r_pack)):
        v = np.ascontiguousarray(v)
        arrays[f"in_{name}"] = v
        args.append(nc.dram_tensor(f"in_{name}", v.shape, mb.dt.from_np(v.dtype), kind="ExternalInput").ap())
    args.append(nc.dram_tensor("out_0", (B, SEQ, D), mb.dt.float32, kind="ExternalOutput").ap())
    two_layer_kernel(nc, *args)
    r = run_bass_kernel_spmd(nc, [arrays], core_ids=[0])
    return r.results[0]["out_0"]
```
